# Optimizing a Trainium2 kernel written in Bass

```python
import numpy as np
import jax
import jax.numpy as jnp

def _softmax(x, axis=-1):
    return jax.nn.softmax(x, axis=axis)
def _gelu(x):
    return jax.nn.gelu(x, approximate=True)
def _silu(x):
    return jax.nn.silu(x)
def _sigmoid(x):
    return jax.nn.sigmoid(x)
def _layernorm(x, axis=-1, eps=1e-5):
    m = jnp.mean(x, axis=axis, keepdims=True)
    v = jnp.var(x, axis=axis, keepdims=True)
    return (x - m) / jnp.sqrt(v + eps)
def _scatter_add(tgt, idx, src, axis=0):
    return tgt.at[idx].add(src)
def _segment_sum(src, seg, n):
    return jax.ops.segment_sum(src, seg, n)

kernel_name = 'mk_metaformer_d1_conv_nhwc128_74a292'

def setup_inputs(seed: int = 0):
    np.random.seed(seed)
    _w = jnp.asarray
    def _rec_inputs():
        import jax
        import jax.numpy as jnp
        _gk = jax.random.key(seed)
        x = -0.0003482 + 1 * jax.random.normal(jax.random.fold_in(_gk, 1), (1, 384, 384, 128), jnp.float32)
        return x
    x = _rec_inputs()
    def _L0_conv_setup():
        import jax, jax.numpy as jnp
        import numpy as np
        B, N, C, M = (1, 384, 128, 128)
        EPS = 1e-05

        def _ln(x, g, b):
            mu = jnp.mean(x, axis=-1, keepdims=True)
            var = jnp.mean(jnp.square(x - mu), axis=-1, keepdims=True)
            return (x - mu) * jax.lax.rsqrt(var + EPS) * g + b
        key = jax.random.key(seed)
        ks = jax.random.split(key, 12)
        s = 0.02
        return {'act': jax.random.normal(ks[0], (B, N, N, C), dtype=jnp.float32), 'mask': jnp.ones((B, N, N), dtype=jnp.float32), 'ln_g': jnp.ones((C,), jnp.float32), 'ln_b': jnp.zeros((C,), jnp.float32), 'Wl': s * jax.random.normal(ks[1], (C, M)), 'bl': jnp.zeros((M,)), 'Wr': s * jax.random.normal(ks[2], (C, M)), 'br': jnp.zeros((M,)), 'Wgl': s * jax.random.normal(ks[3], (C, M)), 'bgl': jnp.zeros((M,)), 'Wgr': s * jax.random.normal(ks[4], (C, M)), 'bgr': jnp.zeros((M,)), 'cg': jnp.ones((M,), jnp.float32), 'cb': jnp.zeros((M,), jnp.float32), 'Wo': s * jax.random.normal(ks[5], (M, C)), 'bo': jnp.zeros((C,)), 'Wg': s * jax.random.normal(ks[6], (C, C)), 'bg': jnp.zeros((C,))}
    _L0_conv_all = _L0_conv_setup()
    _L0_conv_in = {k: v for k, v in _L0_conv_all.items() if k in ('mask', 'ln_g', 'ln_b', 'Wl', 'bl', 'Wr', 'br', 'Wgl', 'bgl', 'Wgr', 'bgr', 'cg', 'cb', 'Wo', 'bo', 'Wg', 'bg', )}
    del _L0_conv_all

    def _L0_ffn_setup():
        import jax, jax.numpy as jnp
        import numpy as np
        B, S, D, E, H, O, K = (512, 2048, 128, 64, 512, 128, 8)
        key = jax.random.key(seed)
        k0, k1, k2, k3 = jax.random.split(key, 4)
        x = jax.random.normal(k0, (B, S, D), dtype=jnp.float32)
        gate_w = jax.random.normal(k1, (E, D), dtype=jnp.float32) * (1.0 / np.sqrt(D))
        gate_b = jnp.zeros((E,), dtype=jnp.float32)
        weight1 = jax.random.uniform(k2, (E, D + 1, H), dtype=jnp.float32, minval=-1.0, maxval=1.0) * (1.0 / np.sqrt(D + 1))
        weight2 = jax.random.uniform(k3, (E, H + 1, O), dtype=jnp.float32, minval=-1.0, maxval=1.0) * (1.0 / np.sqrt(H + 1))
        return {'x': x, 'gate_w': gate_w, 'gate_b': gate_b, 'weight1': weight1, 'weight2': weight2}
    _L0_ffn_all = _L0_ffn_setup()
    _L0_ffn_in = {k: v for k, v in _L0_ffn_all.items() if k in ('gate_w', 'gate_b', 'weight1', 'weight2', )}
    del _L0_ffn_all

    return {
        "x": x,
        "L0_conv_mask": _L0_conv_in["mask"],
        "L0_conv_ln_g": _L0_conv_in["ln_g"],
        "L0_conv_ln_b": _L0_conv_in["ln_b"],
        "L0_conv_Wl": _L0_conv_in["Wl"],
        "L0_conv_bl": _L0_conv_in["bl"],
        "L0_conv_Wr": _L0_conv_in["Wr"],
        "L0_conv_br": _L0_conv_in["br"],
        "L0_conv_Wgl": _L0_conv_in["Wgl"],
        "L0_conv_bgl": _L0_conv_in["bgl"],
        "L0_conv_Wgr": _L0_conv_in["Wgr"],
        "L0_conv_bgr": _L0_conv_in["bgr"],
        "L0_conv_cg": _L0_conv_in["cg"],
        "L0_conv_cb": _L0_conv_in["cb"],
        "L0_conv_Wo": _L0_conv_in["Wo"],
        "L0_conv_bo": _L0_conv_in["bo"],
        "L0_conv_Wg": _L0_conv_in["Wg"],
        "L0_conv_bg": _L0_conv_in["bg"],
        "L0_ffn_gate_w": _L0_ffn_in["gate_w"],
        "L0_ffn_gate_b": _L0_ffn_in["gate_b"],
        "L0_ffn_weight1": _L0_ffn_in["weight1"],
        "L0_ffn_weight2": _L0_ffn_in["weight2"],
    }

def reference(x, L0_conv_mask, L0_conv_ln_g, L0_conv_ln_b, L0_conv_Wl, L0_conv_bl, L0_conv_Wr, L0_conv_br, L0_conv_Wgl, L0_conv_bgl, L0_conv_Wgr, L0_conv_bgr, L0_conv_cg, L0_conv_cb, L0_conv_Wo, L0_conv_bo, L0_conv_Wg, L0_conv_bg, L0_ffn_gate_w, L0_ffn_gate_b, L0_ffn_weight1, L0_ffn_weight2):
    import jax
    import jax.numpy as jnp
    def _L0_conv_ref(act, mask, ln_g, ln_b, Wl, bl, Wr, br, Wgl, bgl, Wgr, bgr, cg, cb, Wo, bo, Wg, bg):
        import jax, jax.numpy as jnp
        import numpy as np
        B, N, C, M = (1, 384, 128, 128)
        EPS = 1e-05

        def _ln(x, g, b):
            mu = jnp.mean(x, axis=-1, keepdims=True)
            var = jnp.mean(jnp.square(x - mu), axis=-1, keepdims=True)
            return (x - mu) * jax.lax.rsqrt(var + EPS) * g + b
        x = _ln(act, ln_g, ln_b)
        m = mask[..., None]
        left = m * (x @ Wl + bl) * jax.nn.sigmoid(x @ Wgl + bgl)
        right = m * (x @ Wr + br) * jax.nn.sigmoid(x @ Wgr + bgr)
        gate = jax.nn.sigmoid(x @ Wg + bg)
        out = jnp.einsum('bikc,bjkc->bijc', left, right)
        out = _ln(out, cg, cb)
        out = (out @ Wo + bo) * gate
        return out

    def _L0_ffn_ref(x, gate_w, gate_b, weight1, weight2):
        import jax, jax.numpy as jnp
        import numpy as np
        B, S, D, E, H, O, K = (512, 2048, 128, 64, 512, 128, 8)
        Bn, Sn, Dn = x.shape
        logits = jnp.einsum('bsd,ed->bse', x, gate_w) + gate_b
        probs = jax.nn.softmax(logits, axis=1)
        vals, idx = jax.lax.top_k(probs.transpose(0, 2, 1), K)
        topv = vals.transpose(0, 2, 1)
        topi = idx.transpose(0, 2, 1)
        flat_idx = topi.reshape(Bn, K * E)
        gathered = jnp.take_along_axis(x, flat_idx[:, :, None], axis=1)
        gathered = gathered.reshape(Bn, K, E, Dn)
        pooled = jnp.einsum('bked,bke->bed', gathered, topv)
        ones = jnp.ones((E, Bn, 1), dtype=x.dtype)
        h = jnp.concatenate([pooled.transpose(1, 0, 2), ones], axis=-1)
        h = jax.nn.gelu(jnp.einsum('ebd,edh->ebh', h, weight1), approximate=False)
        h = jnp.concatenate([h, ones], axis=-1)
        out = jnp.einsum('ebh,eho->ebo', h, weight2)
        out = out.transpose(1, 0, 2)
        weighted = jnp.einsum('beo,bke->bkeo', out, topv).reshape(Bn, K * E, O)
        outputs = jnp.zeros((Bn, Sn, O), dtype=x.dtype)
        outputs = outputs.at[jnp.arange(Bn)[:, None], flat_idx].add(weighted)
        return outputs

    def _gn(v, G=32, eps=1e-5):
        B_, H_, W_, C_ = v.shape
        g = v.reshape(B_, H_, W_, G, C_ // G)
        m = jnp.mean(g, axis=(1, 2, 4), keepdims=True)
        s = jnp.var(g, axis=(1, 2, 4), keepdims=True)
        return ((g - m) / jnp.sqrt(s + eps)).reshape(v.shape)

    def _ln_c(v, eps=1e-6):
        m = jnp.mean(v, axis=-1, keepdims=True)
        s = jnp.var(v, axis=-1, keepdims=True)
        return (v - m) / jnp.sqrt(s + eps)

    def _ln_t(v, eps=1e-5):
        m = jnp.mean(v, axis=-1, keepdims=True)
        s = jnp.var(v, axis=-1, keepdims=True)
        return (v - m) / jnp.sqrt(s + eps)

    def _to_tokens(v):
        B_, H_, W_, C_ = v.shape
        return v.reshape(B_, H_ * W_, C_)
    def _from_tokens(t, like):
        return t.reshape(like.shape)

    x = x + _L0_conv_ref(_ln_c(x), L0_conv_mask, L0_conv_ln_g, L0_conv_ln_b, L0_conv_Wl, L0_conv_bl, L0_conv_Wr, L0_conv_br, L0_conv_Wgl, L0_conv_bgl, L0_conv_Wgr, L0_conv_bgr, L0_conv_cg, L0_conv_cb, L0_conv_Wo, L0_conv_bo, L0_conv_Wg, L0_conv_bg)
    t = _to_tokens(x)
    t = t + _L0_ffn_ref(_ln_t(t), L0_ffn_gate_w, L0_ffn_gate_b, L0_ffn_weight1, L0_ffn_weight2)
    x = _from_tokens(t, x)
    return x


_drawn_inputs = setup_inputs


def setup_inputs(seed=0):
    import zlib

    import numpy as np

    out = dict(_drawn_inputs(seed))
    spreads = {'L0_conv_ln_g': (1.0, 0.6),
     'L0_conv_ln_b': (0.0, 0.1),
     'L0_conv_bl': (0.0, 0.1),
     'L0_conv_br': (0.0, 0.1),
     'L0_conv_bgl': (0.0, 0.8),
     'L0_conv_bgr': (0.0, 0.8),
     'L0_conv_cg': (1.0, 0.6),
     'L0_conv_cb': (0.0, 0.756),
     'L0_conv_bo': (0.0, 0.1),
     'L0_conv_bg': (0.0, 0.8),
     'L0_ffn_gate_b': (0.0, 0.1)}
    factors = {'L0_conv_Wgl': 8.0,
     'L0_conv_Wgr': 8.0,
     'L0_conv_Wg': 3.991,
     'L0_ffn_gate_w': 8.0,
     'L0_ffn_weight1': 8.0,
     'L0_ffn_weight2': 8.0}
    for name, (base, spread) in spreads.items():
        noise = np.random.default_rng([zlib.crc32(name.encode()), seed]).standard_normal(out[name].shape)
        drawn = base * np.exp(spread * noise) if base else spread * noise
        out[name] = jnp.asarray(drawn.astype(out[name].dtype))
    for name, factor in factors.items():
        out[name] = (out[name] * factor).astype(out[name].dtype)
    return out
```

```python
import concourse.bass as bass
from concourse import mybir
from contextlib import ExitStack

F32 = mybir.dt.float32
F32R = mybir.dt.float32r
U32 = mybir.dt.uint32
ALU = mybir.AluOpType
ACT = mybir.ActivationFunctionType
AX = mybir.AxisListType

N = 384
C = 128
E, H, O, K = 64, 512, 128, 8
P = 128
T = N // P
TOKENS = N * N
HC = H // P

CW = 8
CG = C // CW
IB = 16
NB = N // IB

U = 8
Q = N // U

CONV_EPS1, CONV_EPS2 = 1e-6, 1e-5
LN_EPS = 1e-5

HALF = N // 2
GROUP = 4
GT = GROUP // 2 * N
NG = N // GROUP


def after(eng, sem, count):
    if isinstance(count, int) and count <= 0:
        return
    eng.wait_ge(sem, count)


class Row:

    def __init__(self, q, k):
        self.q, self.k = q, k

    def __add__(self, rows):
        return Row(self.q + (self.k + rows) // U, (self.k + rows) % U)

    def __sub__(self, rows):
        return self + -rows

    def number(self, more=0):
        return self.q * U + (self.k + more)

    def tiles(self, more):
        return self.q * (U * T) + (self.k * T + more)

    def group(self, more=0):
        return self.q * (U // GROUP) + (self.k // GROUP + more)

    def exists(self):
        return not isinstance(self.q, int) or 0 <= self.number() < N


def rows_of_loop(eng, step, lead, first=1):
    for n in range(-lead, first * U):
        step(Row(n // U, n % U))
    with eng.Fori(first, Q - 1) as q:
        for k in range(U):
            step(Row(q, k))
    for n in range(N - U, N + U):
        step(Row(n // U, n % U))


def mk_metaformer(nc, x, mask, ln_g, ln_b, Wl, bl, Wr, br, Wgl, bgl, Wgr, bgr, cg, cb, Wo, bo, Wg, bg,
                  gate_w, gate_b, weight1, weight2, out):
    left_d = nc.dram_tensor("left_scratch", [CG, T, P, NB, IB * CW], F32).ap()
    right_d = nc.dram_tensor("right_scratch", [CG, T, P, NB, CW * IB], F32).ap()
    prod_d = nc.dram_tensor("product_scratch", [C, N, N], F32).ap()

    x_rows = x.rearrange("a i (p t) c -> (a i) p (t c)", t=T)
    out_rows = out.rearrange("a i (p t) c -> (a i) p (t c)", t=T)
    out_tokens = out.rearrange("a i j c -> (a i j) c")

    with ExitStack() as keep:
        def tensors(stack):
            def sb(name, shape, dt=F32):
                return stack.enter_context(nc.sbuf_tensor(name, shape, dt))

            def pb(name, shape, dt=F32):
                return stack.enter_context(nc.psum_tensor(name, shape, dt))

            def sem(name):
                return stack.enter_context(nc.semaphore(name))
            return sb, pb, sem

        sb, _, _ = tensors(keep)
        ident = sb("ident", [P, P])
        w_hi = sb("w_hi", [C, 4 * C], F32R)
        w_lo = sb("w_lo", [C, 4 * C], F32R)
        wg_c = sb("wg_c", [C, C])
        wo_c = sb("wo_c", [C, C])
        bo_bc = sb("bo_bc", [P, C])
        gate_wT = sb("gate_wT", [C, E])
        gate_b2 = sb("gate_b2", [P, 1])
        x_scale = sb("x_scale", [P, N, T])
        x_shift = sb("x_shift", [P, N, T])
        mask_T = sb("mask_T", [P, T, N])
        cand_v = sb("cand_v", [P, NG, K])
        cand_i = sb("cand_i", [P, NG, K])
        exp_sum = sb("exp_sum", [P, NG])

        prepare(nc, tensors, ident, w_hi, w_lo, wg_c, wo_c, bo_bc, gate_wT, gate_b2, mask_T,
                mask, ln_g, ln_b, (Wl, Wr, Wgl, Wgr, Wg), (bl, br, bgl, bgr, bg), cg, cb, Wo, bo, gate_w, gate_b)
        project(nc, tensors, x_rows, left_d, right_d, ident, w_hi, w_lo, mask_T, x_scale, x_shift)
        multiply(nc, tensors, left_d, right_d, prod_d)
        finish_rows(nc, tensors, x_rows, out_rows, prod_d, ident, wg_c, wo_c, bo_bc, gate_wT, gate_b2,
                    x_scale, x_shift, cand_v, cand_i, exp_sum)
        experts(nc, tensors, out_tokens, ident, cand_v, cand_i, exp_sum, weight1, weight2)


def prepare(nc, tensors, ident, w_hi, w_lo, wg_c, wo_c, bo_bc, gate_wT, gate_b2, mask_T,
            mask, ln_g, ln_b, weights, biases, cg, cb, Wo, bo, gate_w, gate_b):
    NW = 5 * C
    column = "(c o) -> c o"
    with ExitStack() as stack:
        sb, pb, sem = tensors(stack)
        w_all = sb("w_all", [C, NW])
        wo_raw = sb("wo_raw", [C, C])
        gw_raw = sb("gw_raw", [E, C])
        mask_raw = sb("mask_raw", [P, T, N])
        g_col = sb("g_col", [C, 1])
        b_col = sb("b_col", [C, 1])
        cg_col = sb("cg_col", [C, 1])
        cb_col = sb("cb_col", [C, 1])
        b_row = sb("b_row", [1, NW])
        bo_row = sb("bo_row", [1, C])
        one_row = sb("one_row", [1, P])
        ones = sb("ones", [P, P])
        minus = sb("minus", [P, P])
        b_wide = sb("b_wide", [C, P])
        cb_wide = sb("cb_wide", [C, P])
        wp = sb("wp", [C, NW])
        wop = sb("wop", [C, C])
        wc = sb("wc", [C, NW])
        ps_a = pb("ps_a", [P, 4 * C])
        ps_b = pb("ps_b", [P, C])
        ps_o = pb("ps_o", [P, C])
        ps_bo = pb("ps_bo", [P, C])
        ps_g = pb("ps_g", [C, E])
        ps_m = [pb(f"ps_m{n}", [P, N]) for n in range(2)]
        loaded = sem("prep_loaded")
        ident_done = sem("prep_ident")
        vec = sem("prep_vec")
        folded = sem("prep_folded")
        pe_done = sem("prep_pe")
        mask_pe = sem("prep_mask_pe")
        mask_cp = sem("prep_mask_cp")
        LOADS = 2 * len(weights) + 10
        block = stack.enter_context(nc.Block())

        @block.sync
        def _(sp):
            n = 0
            for at, w in enumerate(weights):
                sp.dma_start(w_all[:, at * C:(at + 1) * C], w).then_inc(loaded, 16)
                sp.dma_start(b_row[0:1, at * C:(at + 1) * C],
                             biases[at].rearrange("(o c) -> o c", o=1)).then_inc(loaded, 16)
                n += 2
            for dst, src in ((wo_raw[:], Wo), (gw_raw[:], gate_w),
                             (mask_raw[:], mask.rearrange("a (r p) j -> p (a r) j", p=P)),
                             (bo_row[:], bo.rearrange("(o c) -> o c", o=1)),
                             (g_col[:], ln_g.rearrange(column, o=1)), (b_col[:], ln_b.rearrange(column, o=1)),
                             (cg_col[:], cg.rearrange(column, o=1)), (cb_col[:], cb.rearrange(column, o=1)),
                             (gate_b2[0:E, :], gate_b.rearrange(column, o=1)),
                             (gate_b2[E:2 * E, :], gate_b.rearrange(column, o=1))):
                sp.dma_start(dst, src).then_inc(loaded, 16)
                n += 1
            assert n == LOADS

        @block.gpsimd
        def _(pool):
            pool.memset(ident[:], 0.0).then_inc(ident_done, 1)
            pool.wait_ge(ident_done, 1)
            pool.affine_select(out=ident[:], in_=ident[:], compare_op=ALU.not_equal, fill=1.0,
                               base=0, pattern=[[-1, P]], channel_multiplier=1).then_inc(ident_done, 1)

        @block.vector
        def _(dve):
            dve.memset(ones[:], 1.0)
            dve.memset(minus[:], -1.0)
            dve.memset(one_row[:], 1.0).then_inc(vec, 1)
            dve.wait_ge(vec, 1)
            dve.wait_ge(loaded, 16 * LOADS)
            dve.tensor_scalar(b_wide[:], ones[:], b_col[:], None, ALU.mult)
            dve.tensor_scalar(cb_wide[:], ones[:], cb_col[:], None, ALU.mult)
            dve.tensor_scalar(wp[:], w_all[:], g_col[:], None, ALU.mult)
            dve.tensor_scalar(wop[:], wo_raw[:], cg_col[:], None, ALU.mult).then_inc(folded, 1)
            dve.wait_ge(pe_done, 1)
            dve.scalar_tensor_tensor(wc[:, 0:4 * C], ps_a[:], 1.0 / C, wp[:, 0:4 * C], ALU.mult, ALU.add)
            dve.scalar_tensor_tensor(wg_c[:], ps_b[:], 1.0 / C, wp[:, 4 * C:], ALU.mult, ALU.add)
            dve.scalar_tensor_tensor(wo_c[:], ps_o[:], 1.0 / C, wop[:], ALU.mult, ALU.add)
            dve.tensor_copy(bo_bc[:], ps_bo[:])
            dve.tensor_copy(gate_wT[:], ps_g[:]).then_inc(vec, 1)
            dve.wait_ge(vec, 2)
            dve.tensor_copy(w_hi[:], wc[:, 0:4 * C]).then_inc(vec, 1)
            dve.wait_ge(vec, 3)
            dve.tensor_tensor(w_lo[:], wc[:, 0:4 * C], w_hi[:].bitcast(F32), ALU.subtract)
            for t in range(T):
                dve.wait_ge(mask_pe, t + 1)
                dve.tensor_copy(mask_T[:, t, :], ps_m[t % 2][:]).then_inc(mask_cp, 1)

        @block.tensor
        def _(pe):
            pe.wait_ge(ident_done, 2)
            pe.wait_ge(folded, 1)
            pe.matmul(ps_a[:], minus[:], wp[:, 0:4 * C], start=True, stop=False)
            pe.matmul(ps_a[:], b_wide[:], w_all[:, 0:4 * C], start=False, stop=False)
            pe.matmul(ps_a[:], one_row[:], b_row[0:1, 0:4 * C], start=False, stop=True)
            pe.matmul(ps_b[:], minus[:], wp[:, 4 * C:], start=True, stop=False)
            pe.matmul(ps_b[:], b_wide[:], w_all[:, 4 * C:], start=False, stop=False)
            pe.matmul(ps_b[:], one_row[:], b_row[0:1, 4 * C:], start=False, stop=True)
            pe.matmul(ps_o[:], minus[:], wop[:], start=True, stop=True)
            pe.matmul(ps_bo[:], cb_wide[:], wo_raw[:], start=True, stop=False)
            pe.matmul(ps_bo[:], one_row[:], bo_row[:], start=False, stop=True)
            pe.transpose(ps_g[:], gw_raw[:], ident[0:E, 0:E]).then_inc(pe_done, 1)
            for t in range(T):
                if t >= 2:
                    pe.wait_ge(mask_cp, t - 1)
                for r in range(T):
                    last = pe.transpose(ps_m[t % 2][:, r * P:(r + 1) * P], mask_raw[:, r, t::T], ident[:])
                last.then_inc(mask_pe, 1)


def norm_moments(pool, st, s, n):
    pool.tensor_tensor(s[:, 0, 0:n], st[:, :, 1], st[:, :, 4], ALU.add)
    pool.tensor_tensor(s[:, 1, 0:n], st[:, :, 1], st[:, :, 4], ALU.subtract)
    pool.tensor_tensor(s[:, 2, 0:n], st[:, :, 2], st[:, :, 5], ALU.add)
    pool.drain()


def norm_scale(pool, s, n, gain, eps, minus_half):
    pool.tensor_tensor(s[:, 1, 0:n], s[:, 1, 0:n], s[:, 1, 0:n], ALU.mult)
    pool.tensor_scalar(s[:, 2, 0:n], s[:, 2, 0:n], gain / C, eps, ALU.mult, ALU.add)
    pool.drain()
    pool.tensor_scalar(s[:, 1, 0:n], s[:, 1, 0:n], gain / 4, 0.0, ALU.mult, ALU.add)
    pool.drain()
    pool.tensor_tensor(s[:, 2, 0:n], s[:, 2, 0:n], s[:, 1, 0:n], ALU.add)
    pool.drain()
    pool.tensor_tensor(s[:, 3, 0:n], s[:, 2, 0:n], minus_half[:, 0:n], ALU.pow)
    pool.drain()


def project(nc, tensors, x_rows, left_d, right_d, ident, w_hi, w_lo, mask_T, x_scale, x_shift):
    AHEAD_STATS, AHEAD_T, AHEAD_SPLIT = 4, 2, 1
    with ExitStack() as stack:
        sb, pb, sem = tensors(stack)
        xin = sb("xin", [P, U, T * C])
        st = sb("st", [P, U, T, 6])
        small = sb("small", [P, U // 2, 5, 2 * T])
        minus_half = sb("minus_half", [P, 2 * T])
        xn = sb("xn", [P, U, T, C])
        xT_hi = [sb(f"xT_hi{n}", [C, N], F32R) for n in range(2)]
        xT_lo = [sb(f"xT_lo{n}", [C, N], F32R) for n in range(2)]
        gates = sb("gates", [P, 2 * T, 2 * C])
        stage_l = sb("stage_l", [P, 2, T, CG, IB, CW])
        stage_r = sb("stage_r", [P, 2, T, CG, CW, IB])
        ps_x = [pb(f"ps_x{n}", [C, N]) for n in range(2)]
        ps_w = [pb(f"ps_w{n}", [P, 4 * C]) for n in range(2 * T)]
        x_loaded = [sem(f"x_loaded{n}") for n in range(U // 2)]
        half_set = sem("half_set")
        stats_done = sem("p1_stats")
        xn_done = sem("p1_xn")
        xT_done = sem("p1_xT")
        hi_done = sem("p1_hi")
        lo_done = sem("p1_lo")
        proj_done = sem("p1_proj")
        sig_done = sem("p1_sig")
        gated = sem("p1_gated")
        stored = [sem(f"p1_stored{n}") for n in range(2)]
        block = stack.enter_context(nc.Block())

        @block.sync
        def _(sp):
            def load(pair, k):
                after(sp, xn_done, 2 * pair - U + 2)
                sp.dma_start(xin[:, 2 * k:2 * k + 2, :],
                             x_rows[bass.ds(pair * 2, 2)].rearrange("r p n -> p r n")).then_inc(x_loaded[k], 16)

            PAIRS = IB // 2
            AHEAD = U // 2

            def store(b, buf):
                sp.wait_ge(gated, (b + 1) * IB * T)
                for t in range(T):
                    for src, dst in ((stage_l, left_d), (stage_r, right_d)):
                        sp.dma_start(dst[:, t, :, bass.ds(b, 1), :].rearrange("g p b n -> p g (b n)"),
                                     src[:, buf, t].rearrange("p g a b -> p g (a b)")).then_inc(stored[buf], 16)

            for pair in range(AHEAD):
                load(pair, pair)
            for b in range(2):
                for j in range(PAIRS):
                    load(b * PAIRS + j + AHEAD, j % AHEAD)
                store(b, b)
            with sp.Fori(1, NB // 2 - 1) as bb:
                for buf in range(2):
                    for j in range(PAIRS):
                        load((bb * 2 + buf) * PAIRS + j + AHEAD, j % AHEAD)
                    store(bb * 2 + buf, buf)
            for b in range(NB - 2, NB):
                for j in range(PAIRS):
                    if b * PAIRS + j + AHEAD < N // 2:
                        load(b * PAIRS + j + AHEAD, j % AHEAD)
                store(b, b % 2)
            for buf in range(2):
                sp.wait_ge(stored[buf], 16 * 2 * T * (NB // 2))

        @block.vector
        def _(dve):
            dve.memset(minus_half[:], -0.5).then_inc(half_set, 1)

            def stats(row):
                k = row.k
                dve.wait_ge(x_loaded[k // 2], (row.q + 1) * 16)
                for t in range(T):
                    last = dve.bn_stats(st[:, k, t, :], xin[:, k, t * C:(t + 1) * C])
                last.then_inc(stats_done, 1)

            def split(row):
                k = row.k
                dve.wait_ge(hi_done, row.number(1))
                par = k % 2
                dve.tensor_tensor(xT_lo[par][:], ps_x[par][:], xT_hi[par][:].bitcast(F32),
                                  ALU.subtract).then_inc(lo_done, 1)

            def gate(row):
                k = row.k
                q = row.q
                buf, ii = (q // (IB // U)) % 2, (q % (IB // U)) * U + k
                if k == 0:
                    after(dve, stored[0], q // (2 * IB // U) * (16 * 2 * T))
                    after(dve, stored[1], (q - IB // U) // (2 * IB // U) * (16 * 2 * T))
                for t in range(T):
                    tile = k % 2 * T + t
                    dve.wait_ge(sig_done, row.tiles(t + 1))
                    dst_l = stage_l[:, bass.ds(buf, 1), t, :, bass.ds(ii, 1), :].rearrange("p b g i c -> p (b g) (i c)")
                    dst_r = stage_r[:, bass.ds(buf, 1), t, :, :, bass.ds(ii, 1)].rearrange("p b g c i -> p (b g) (c i)")
                    for side, dst in enumerate((dst_l, dst_r)):
                        cols = slice(side * C, (side + 1) * C)
                        last = dve.scalar_tensor_tensor(
                            dst, ps_w[tile][:, cols].rearrange("p (g c) -> p g c", g=CG),
                            mask_T[:, t, bass.ds(row.number(), 1)],
                            gates[:, tile, cols].rearrange("p (g c) -> p g c", g=CG), ALU.mult, ALU.mult)
                    last.then_inc(gated, 1)

            def step(row):
                if (row + AHEAD_SPLIT).exists():
                    split(row + AHEAD_SPLIT)
                if row.exists():
                    gate(row)
                if (row + AHEAD_STATS).exists():
                    stats(row + AHEAD_STATS)

            rows_of_loop(dve, step, AHEAD_STATS, first=2)

        @block.gpsimd
        def _(pool):
            pool.wait_ge(half_set, 1)

            def normalise(row):
                k = row.k
                """Rows row and row + 1: their scales, then (x - mean) / std + 1."""
                s = small[:, k // 2]
                after(pool, stats_done, row.number(2))
                norm_moments(pool, st[:, k:k + 2].rearrange("p r t s -> p (r t) s"), s, 2 * T)
                norm_scale(pool, s, 2 * T, 1.0 + CONV_EPS2, CONV_EPS1 * CONV_EPS2, minus_half)
                pool.tensor_tensor(s[:, 0], s[:, 0], s[:, 3], ALU.mult)
                pool.drain()
                pool.tensor_scalar(s[:, 4], s[:, 0], -0.5, 1.0, ALU.mult, ALU.add)
                pool.drain()
                after(pool, xT_done, row.number(-U + 2))
                for t in range(2 * T):
                    if t == 0:
                        pool.tensor_copy(x_scale[:, bass.ds(row.number(), 2), :],
                                         s[:, 3].rearrange("p (r t) -> p r t", t=T))
                        pool.tensor_copy(x_shift[:, bass.ds(row.number(), 2), :],
                                         s[:, 4].rearrange("p (r t) -> p r t", t=T))
                    last = pool.tensor_scalar(xn[:, k + t // T, t % T, :],
                                              xin[:, k + t // T, (t % T) * C:(t % T + 1) * C],
                                              s[:, 3, t:t + 1], s[:, 4, t:t + 1], ALU.mult, ALU.add)
                    if t % T == T - 1:
                        last.then_inc(xn_done, 1)

            def step(row):
                k = row.k
                if (row + AHEAD_STATS).exists() and k % 2 == 0:
                    normalise(row + AHEAD_STATS)

            rows_of_loop(pool, step, AHEAD_STATS)

        @block.tensor
        def _(pe):
            def transposes(row):
                k = row.k
                pe.wait_ge(xn_done, row.number(1))
                after(pe, lo_done, row.number(-1))
                for t in range(T):
                    last = pe.transpose(ps_x[k % 2][:, t * P:(t + 1) * P], xn[:, k, t, :], ident[:])
                last.then_inc(xT_done, 1)

            def projections(row):
                k = row.k
                hi, lo = xT_hi[k % 2], xT_lo[k % 2]
                pe.wait_ge(lo_done, row.number(1))
                for t in range(T):
                    dst = ps_w[k % 2 * T + t]
                    at = slice(t * P, (t + 1) * P)
                    after(pe, gated, row.tiles(t + 1 - 2 * T))
                    pe.matmul(dst[:], hi[:, at], w_hi[:], start=True, stop=False)
                    pe.matmul(dst[:], hi[:, at], w_lo[:], start=False, stop=False)
                    pe.matmul(dst[:], lo[:, at], w_hi[:], start=False, stop=True).then_inc(proj_done, 1)

            def step(row):
                if (row + AHEAD_T).exists():
                    transposes(row + AHEAD_T)
                if row.exists():
                    projections(row)

            rows_of_loop(pe, step, AHEAD_T)

        @block.scalar
        def _(act):
            def upper(row):
                k = row.k
                act.wait_ge(xT_done, row.number(1))
                after(act, proj_done, row.tiles(-T))
                act.activation(xT_hi[k % 2][:], ps_x[k % 2][:], ACT.Copy).then_inc(hi_done, 1)

            def sigmoids(row):
                k = row.k
                for t in range(T):
                    tile = k % 2 * T + t
                    act.wait_ge(proj_done, row.tiles(t + 1))
                    act.activation(gates[:, tile, :], ps_w[tile][:, 2 * C:4 * C],
                                   ACT.Sigmoid).then_inc(sig_done, 1)

            def step(row):
                if (row + AHEAD_SPLIT).exists():
                    upper(row + AHEAD_SPLIT)
                if row.exists():
                    sigmoids(row)

            rows_of_loop(act, step, AHEAD_SPLIT)


def multiply(nc, tensors, left_d, right_d, prod_d):
    SLOTS = 3
    V = 2 * SLOTS
    RT = N // P
    with ExitStack() as stack:
        sb, pb, sem = tensors(stack)
        left = sb("left", [P, 2, T, N, CW])
        right = sb("right", [P, 2, T, NB, CW, IB])
        prod = sb("prod", [P, SLOTS, RT, N])
        ps = [pb(f"ps_p{n}", [P, N]) for n in range(2 * RT)]
        loaded = [sem(f"p2_loaded{n}") for n in range(2)]
        summed = sem("p2_summed")
        copied = sem("p2_copied")
        stored = [sem(f"p2_stored{n}") for n in range(SLOTS)]
        block = stack.enter_context(nc.Block())
        PER = CW * RT

        @block.sync
        def _(sp):
            def load(g, buf):
                after(sp, summed, (g - 1) * PER)
                for dst, src in ((left[:, buf].rearrange("p t i c -> p t (i c)"), left_d),
                                 (right[:, buf].rearrange("p t b c i -> p t (b c i)"), right_d)):
                    sp.dma_start(dst,
                                 src[bass.ds(g, 1)].rearrange("g t p b n -> p (g t) (b n)")
                                 ).then_inc(loaded[buf], 16)

            load(0, 0)
            load(1, 1)
            with sp.Fori(1, CG // 2) as gg:
                for buf in range(2):
                    load(gg * 2 + buf, buf)

        @block.tensor
        def _(pe):
            def group(g, visits, buf):
                pe.wait_ge(loaded[buf], (visits + 1) * 32)
                for c in range(CW):
                    for r in range(RT):
                        n = c * RT + r
                        after(pe, copied, g * PER + n - 2 * RT + 1)
                        for t in range(T):
                            last = pe.matmul(ps[n % (2 * RT)][:],
                                             left[:, buf, t, r * P:(r + 1) * P, c],
                                             right[:, buf, t, :, c, :], start=(t == 0), stop=(t == T - 1))
                        last.then_inc(summed, 1)

            group(0, 0, 0)
            group(1, 0, 1)
            with pe.Fori(1, CG // 2) as gg:
                for buf in range(2):
                    group(gg * 2 + buf, gg, buf)

        def channels(eng, step):
            for c in range(V):
                step(c, c)
            with eng.Fori(1, C // V) as m:
                for c in range(V):
                    step(m * V + c, c)
            for c in range(C // V * V, C):
                step(c, c % V)

        @block.vector
        def _(dve):
            def copy(channel, c):
                s, bank = c % SLOTS, c % 2 * RT
                after(dve, stored[s], ((channel - c) // SLOTS + c // SLOTS) * 16)
                for r in range(RT):
                    dve.wait_ge(summed, channel * RT + r + 1)
                    dve.tensor_copy(prod[:, s, r, :], ps[bank + r][:]).then_inc(copied, 1)

            channels(dve, copy)

        @block.scalar
        def _(act):
            def store(channel, c):
                act.wait_ge(copied, (channel + 1) * RT)
                act.dma_start(prod_d[bass.ds(channel, 1)].rearrange("c (r p) j -> p (c r) j", p=P),
                              prod[:, c % SLOTS]).then_inc(stored[c % SLOTS], 16)

            channels(act, store)
            for s in range(SLOTS):
                act.wait_ge(stored[s], 16 * len(range(s, C, SLOTS)))


def finish_rows(nc, tensors, x_rows, out_rows, prod_d, ident, wg_c, wo_c, bo_bc, gate_wT, gate_b2,
                x_scale, x_shift, cand_v, cand_i, exp_sum):
    with ExitStack() as stack:
        sb, pb, sem = tensors(stack)
        prodT = [sb(f"prodT{n}", [C, N]) for n in range(U)]
        xin = sb("x3", [P, U, T * C])
        xs = sb("xs", [P, 2, 2, T])
        xn = sb("xn3", [P, 2, T, C])
        xnT = [sb(f"xnT{n}", [C, N]) for n in range(2)]
        gates = sb("gates3", [P, 2, T * C])
        branch = sb("branch", [P, 2, T * C])
        x1 = sb("x1", [P, U, T * C])
        st = sb("st3", [P, 2, 2, T, 6])
        small = sb("small3", [P, 4, 5, 2 * T])
        minus_half = sb("minus_half3", [P, 2 * T])
        x1n = sb("x1n", [P, 2, T, C])
        x1T = [sb(f"x1T{n}", [C, N]) for n in range(2)]
        logits = sb("logits", [P, 2, GT])
        top_v = sb("top_v", [P, 2, K])
        top_i = sb("top_i", [P, 2, K], U32)
        neg_max = sb("neg_max", [P, 2])
        exps = sb("exps", [P, GT])
        ps_x = pb("ps3_x", [C, N])
        ps_g = pb("ps3_g", [P, N])
        ps_o = [pb(f"ps3_o{n}", [P, N]) for n in range(2)]
        ps_y = [pb(f"ps3_y{n}", [P, N]) for n in range(2)]
        ps_t = pb("ps3_t", [C, N])
        ps_l = pb("ps3_l", [P, N])
        loaded = [sem(f"p3_loaded{n}") for n in range(U)]
        stored = [sem(f"p3_stored{n}") for n in range(U)]
        half_set = sem("p3_half")
        st_set = sem("p3_st")
        xn_done = sem("p3_xn")
        scales_done = sem("p3_scales")
        x1n_done = sem("p3_x1n")
        x1_done = sem("p3_x1")
        xT_done = sem("p3_xT")
        oT_done = sem("p3_oT")
        g_done = sem("p3_g")
        y_done = sem("p3_y")
        x1T_done = sem("p3_x1T")
        l_done = sem("p3_l")
        xcp_done = sem("p3_xcp")
        gate_done = sem("p3_gate")
        x1cp_done = sem("p3_x1cp")
        log_done = sem("p3_log")
        exp_done = sem("p3_exp")
        o_stats = sem("p3_ostats")
        x1_stats = sem("p3_x1stats")
        bias_done = sem("p3_bias")
        gated = sem("p3_gated")
        tops = sem("p3_tops")
        top_sem = sem("p3_top")
        tops_i = sem("p3_tops_i")
        block = stack.enter_context(nc.Block())
        G = U // GROUP

        def image_row(row):
            return row.q * (U // 2) + (row.k // 2 + HALF * (row.k % 2))

        @block.sync
        def _(sp):
            AHEAD = 6

            def load(row):
                k = row.k
                after(sp, y_done, row.number(-U + 1))
                after(sp, x1_done, row.number(-U + 1))
                i = image_row(row)
                sp.dma_start(prodT[k][:], prod_d[:, bass.ds(i, 1), :].rearrange("c i j -> c (i j)")).then_inc(loaded[k], 16)
                sp.dma_start(xin[:, k, :], x_rows[bass.ds(i, 1)].rearrange("i p n -> p (i n)")).then_inc(loaded[k], 16)

            def store(row):
                k = row.k
                sp.wait_ge(x1_done, row.number(1))
                i = image_row(row)
                sp.dma_start(out_rows[bass.ds(i, 1)].rearrange("i p n -> p (i n)"), x1[:, k, :]).then_inc(stored[k], 16)

            def step(row):
                if (row + AHEAD).exists():
                    load(row + AHEAD)
                if row.exists():
                    store(row)

            rows_of_loop(sp, step, AHEAD)
            for k in range(U):
                sp.wait_ge(stored[k], 16 * Q)

        @block.gpsimd
        def _(pool):
            pool.memset(minus_half[:], -0.5).then_inc(half_set, 1)
            pool.wait_ge(half_set, 1)

            def tokens(row):
                k = row.k
                """Normalised tokens + 1, by the scales kept from the projections."""
                pool.wait_ge(loaded[k], (row.q + 1) * 32)
                after(pool, xT_done, row.number(-1))
                i = image_row(row)
                s = xs[:, k % 2]
                pool.tensor_copy(s[:, 0, :], x_scale[:, bass.ds(i, 1), :].rearrange("p i t -> p (i t)"))
                pool.tensor_copy(s[:, 1, :], x_shift[:, bass.ds(i, 1), :].rearrange("p i t -> p (i t)"))
                pool.drain()
                for t in range(T):
                    last = pool.tensor_scalar(xn[:, k % 2, t, :], xin[:, k, t * C:(t + 1) * C],
                                              s[:, 0, t:t + 1], s[:, 1, t:t + 1], ALU.mult, ALU.add)
                last.then_inc(xn_done, 1)

            def scales(row):
                k = row.k
                """Scales of the product of row + 2 and of x1 of row."""
                s = small[:, k % 4]
                if (row + 2).exists():
                    pool.wait_ge(o_stats, row.number(3))
                if row.exists():
                    pool.wait_ge(x1_stats, row.number(1))
                after(pool, x1T_done, row.number(-1))
                after(pool, bias_done, row.number(-1))
                norm_moments(pool, st[:, k % 2].rearrange("p a t s -> p (a t) s"), s, 2 * T)
                norm_scale(pool, s, 2 * T, 1.0, LN_EPS, minus_half)
                pool.tensor_tensor(s[:, 0], s[:, 0], s[:, 3], ALU.mult)
                pool.drain()
                pool.tensor_scalar(s[:, 4], s[:, 0], -0.5, 0.0, ALU.mult, ALU.add).then_inc(scales_done, 1)
                pool.drain()

            def normalise(row):
                k = row.k
                s = small[:, k % 4]
                for t in range(T):
                    last = pool.tensor_scalar(x1n[:, k % 2, t, :], x1[:, k, t * C:(t + 1) * C],
                                              s[:, 3, T + t:T + t + 1], s[:, 4, T + t:T + t + 1], ALU.mult, ALU.add)
                last.then_inc(x1n_done, 1)

            def residual(row):
                k = row.k
                pool.wait_ge(gated, row.number(1))
                after(pool, stored[k], row.q * 16)
                pool.tensor_tensor(x1[:, k, :], branch[:, k % 2, :], xin[:, k, :], ALU.add).then_inc(x1_done, 1)

            def step(row):
                if (row + 2).exists() or row.exists():
                    scales(row)
                if row.exists():
                    normalise(row)
                if (row + 3).exists():
                    tokens(row + 3)
                if (row + 1).exists():
                    residual(row + 1)

            rows_of_loop(pool, step, 3)

        @block.tensor
        def _(pe):
            def tokens(row):
                k = row.k
                pe.wait_ge(xn_done, row.number(1))
                after(pe, xcp_done, row.number())
                for t in range(T):
                    last = pe.transpose(ps_x[:, t * P:(t + 1) * P], xn[:, k % 2, t, :], ident[:])
                last.then_inc(xT_done, 1)

            def product(row):
                k = row.k
                pe.wait_ge(loaded[k], (row.q + 1) * 32)
                after(pe, o_stats, row.number(-1))
                for t in range(T):
                    last = pe.transpose(ps_o[k % 2][:, t * C:(t + 1) * C], prodT[k][:, t::T], ident[:])
                last.then_inc(oT_done, 1)

            def gate(row):
                k = row.k
                pe.wait_ge(xcp_done, row.number(1))
                after(pe, gate_done, row.number())
                for t in range(T):
                    last = pe.matmul(ps_g[:, t * C:(t + 1) * C], xnT[k % 2][:, t * P:(t + 1) * P], wg_c[:],
                                     start=True, stop=True)
                last.then_inc(g_done, 1)

            def outward(row):
                k = row.k
                after(pe, gated, row.number(-1))
                for t in range(T):
                    last = pe.matmul(ps_y[k % 2][:, t * C:(t + 1) * C], prodT[k][:, t::T], wo_c[:],
                                     start=True, stop=True)
                last.then_inc(y_done, 1)

            def tokens1(row):
                k = row.k
                pe.wait_ge(x1n_done, row.number(1))
                after(pe, x1cp_done, row.number())
                for t in range(T):
                    last = pe.transpose(ps_t[:, t * P:(t + 1) * P], x1n[:, k % 2, t, :], ident[:])
                last.then_inc(x1T_done, 1)

            def expert_logits(row):
                k = row.k
                pe.wait_ge(x1cp_done, row.number(1))
                after(pe, log_done, row.number())
                half = k % 2
                pe.matmul(ps_l[half * E:(half + 1) * E, :], gate_wT[:], x1T[k % 2][:],
                          start=True, stop=True).then_inc(l_done, 1)

            def step(row):
                if (row + 2).exists():
                    tokens(row + 2)
                    product(row + 2)
                if (row + 1).exists():
                    gate(row + 1)
                    outward(row + 1)
                if (row - 1).exists():
                    tokens1(row - 1)
                if (row - 2).exists():
                    expert_logits(row - 2)

            rows_of_loop(pe, step, 3)

        @block.scalar
        def _(act):
            def tokens(row):
                k = row.k
                act.wait_ge(xT_done, row.number(1))
                after(act, g_done, row.number(-1))
                act.activation(xnT[k % 2][:], ps_x[:], ACT.Copy).then_inc(xcp_done, 1)

            def gate(row):
                k = row.k
                act.wait_ge(g_done, row.number(1))
                after(act, gated, row.number(-1))
                act.activation(gates[:, k % 2, :], ps_g[:], ACT.Sigmoid).then_inc(gate_done, 1)

            def tokens1(row):
                k = row.k
                act.wait_ge(x1T_done, row.number(1))
                after(act, l_done, row.number(-1))
                act.activation(x1T[k % 2][:], ps_t[:], ACT.Copy).then_inc(x1cp_done, 1)

            def expert_logits(row):
                k = row.k
                half, unit, g = k % 2, k % GROUP // 2, k // GROUP
                act.wait_ge(l_done, row.number(1))
                if k % GROUP < 2:
                    after(act, tops_i, row.group(-1))
                    after(act, exp_done, row.group(-1))
                side = slice(half * E, (half + 1) * E)
                act.activation(logits[side, g, unit * N:(unit + 1) * N].rearrange("e (p t) -> e t p", t=T),
                               ps_l[side, :].rearrange("e (t p) -> e t p", t=T),
                               ACT.Identity, bias=gate_b2[side, :]).then_inc(log_done, 1)

            def exponentials(row):
                k = row.k
                """The group that ended with this row."""
                g, slot = row.group(), row.k // GROUP
                act.wait_ge(tops, g + 1)
                act.wait_ge(tops_i, g + 1)
                act.activation(exps[:], logits[:, slot, :], ACT.Exp, bias=neg_max[:, slot:slot + 1],
                               accum_out=exp_sum[:, bass.ds(g, 1)]).then_inc(exp_done, 1)

            def step(row):
                k = row.k
                if (row + 2).exists():
                    tokens(row + 2)
                if (row + 1).exists():
                    gate(row + 1)
                if (row - 1).exists():
                    tokens1(row - 1)
                if (row - 2).exists():
                    expert_logits(row - 2)
                if (row - 5).exists() and row.k % GROUP == 0:
                    exponentials(row - 5)

            rows_of_loop(act, step, 3)

        @block.vector
        def _(dve):
            dve.memset(st[:], 0.0).then_inc(st_set, 1)
            dve.wait_ge(st_set, 1)

            def x1_records(row):
                k = row.k
                dve.wait_ge(x1_done, row.number(1))
                after(dve, scales_done, row.number(1))
                for t in range(T):
                    last = dve.bn_stats(st[:, k % 2, 1, t, :], x1[:, k, t * C:(t + 1) * C])
                last.then_inc(x1_stats, 1)

            def product_records(row):
                k = row.k
                dve.wait_ge(oT_done, row.number(1))
                after(dve, scales_done, row.number(-1))
                for t in range(T):
                    last = dve.bn_stats(st[:, k % 2, 0, t, :], ps_o[k % 2][:, t * C:(t + 1) * C])
                last.then_inc(o_stats, 1)

            def bias_and_gate(row):
                k = row.k
                dve.wait_ge(y_done, row.number(1))
                dve.wait_ge(scales_done, row.number(1))
                s = small[:, (k - 2) % 4]
                y = ps_y[k % 2]
                for t in range(T):
                    last = dve.scalar_tensor_tensor(y[:, t * C:(t + 1) * C], y[:, t * C:(t + 1) * C],
                                                    s[:, 3, t:t + 1], bo_bc[:], ALU.mult, ALU.add)
                last.then_inc(bias_done, 1)
                dve.wait_ge(bias_done, row.number(1))
                dve.wait_ge(gate_done, row.number(1))
                after(dve, x1_done, row.number(-1))
                dve.tensor_tensor(branch[:, k % 2, :], y[:], gates[:, k % 2, :], ALU.mult).then_inc(gated, 1)

            def largest(row):
                k = row.k
                """The group whose last row is row: its K largest logits and their places."""
                g = row.group()
                slot = k // GROUP
                dve.wait_ge(log_done, row.number(1))
                after(dve, exp_done, g - 1)
                dve.memset(neg_max[:, slot:slot + 1], 0.0)
                dve.max(top_v[:, slot, :], logits[:, slot, :]).then_inc(top_sem, 1)
                dve.wait_ge(top_sem, g + 1)
                dve.tensor_scalar(neg_max[:, slot:slot + 1], top_v[:, slot, 0:1], -1.0, None, ALU.mult).then_inc(tops, 1)
                dve.tensor_copy(cand_v[:, bass.ds(g, 1), :].rearrange("p g k -> p (g k)"), top_v[:, slot, :])
                dve.max_index(top_i[:, slot, :], top_v[:, slot, :], logits[:, slot, :]).then_inc(tops_i, 1)
                dve.wait_ge(tops_i, g + 1)
                dve.tensor_copy(cand_i[:, bass.ds(g, 1), :].rearrange("p g k -> p (g k)"), top_i[:, slot, :])

            def step(row):
                k = row.k
                if row.exists():
                    x1_records(row)
                if (row + 2).exists():
                    product_records(row + 2)
                if (row + 1).exists():
                    bias_and_gate(row + 1)
                if (row - 4).exists() and k % GROUP == GROUP - 1:
                    largest(row - 4)

            rows_of_loop(dve, step, 3)


def experts(nc, tensors, out_tokens, ident, cand_v, cand_i, exp_sum, weight1, weight2):
    EG = 8
    SL = 2
    NC2 = 2 * NG * K
    with ExitStack() as stack:
        sb, pb, sem = tensors(stack)
        w1 = sb("w1", [P, SL, EG, H])
        w2 = sb("w2", [P, SL, EG, HC, O])
        base = sb("base", [P, NG, K])
        mv = sb("mv", [E, 2, NG, K])
        mi = sb("mi", [E, 2, NG, K])
        ms = sb("ms", [E, 2, NG])
        place = sb("place", [E, NC2])
        junk = sb("junk", [E, NC2])
        v8 = sb("v8", [E, K])
        p8 = sb("p8", [E, K], U32)
        p8f = sb("p8f", [E, K])
        idx = sb("idx", [E, K])
        idx_u = sb("idx_u", [E, K], U32)
        negm = sb("negm", [E, 1])
        eg = sb("eg", [E, 2 * NG])
        zsum = sb("zsum", [E, 1])
        zrec = sb("zrec", [E, 1])
        topv = sb("topv", [E, K])
        xg = sb("xg", [E, K, C])
        xgn = sb("xgn", [E, K, C])
        st = sb("st4", [E, K, 6])
        mean_var = sb("mean_var", [E, K, 2])
        half = sb("half4", [E, K])
        var_e = sb("var_e", [E, K])
        rstd = sb("rstd", [E, K])
        nbias = sb("nbias", [E, K])
        pooled = sb("pooled", [E, C])
        pooledT = sb("pooledT", [C, E])
        b1 = sb("b1", [E, H])
        b1T = sb("b1T", [P, HC, E])
        b2 = sb("b2", [E, O])
        h_pre = sb("h_pre", [P, HC, E])
        hT = sb("hT", [P, HC, E])
        oT = sb("oT", [O, E])
        out_e = sb("out_e", [E, O])
        diag = sb("diag", [E, K, E])
        idx_bc = sb("idx_bc", [E, K, E])
        ones = sb("ones4", [E, E])
        lower = sb("lower", [E, E])
        sel = sb("sel", [E, 2, K, E])
        sel_t = sb("sel_t", [E, K, E])
        dup = sb("dup", [E, K])
        idx_s = sb("idx_s", [E, K])
        idx_su = sb("idx_su", [E, K], U32)
        final = sb("final", [E, K, C])
        ps_p = pb("ps4_p", [C, E])
        ps_b = pb("ps4_b", [P, HC * E])
        ps_h = pb("ps4_h", [P, HC * E])
        ps_oT = pb("ps4_oT", [O, E])
        ps_oe = pb("ps4_oe", [E, O])
        ps_i = pb("ps4_i", [E, K * E])
        ps_r = [pb(f"ps4_r{n}", [E, 4 * C]) for n in range(2)]
        w1_in = [sem(f"w1_in{n}") for n in range(SL)]
        w2_in = [sem(f"w2_in{n}") for n in range(SL)]
        b_in = sem("b_in")
        v = sem("p4_v")
        pool_s = sem("p4_pool")
        based = sem("p4_based")
        merged = sem("p4_merged")
        max_s = sem("p4_max")
        exp_s = sem("p4_exp")
        idx_s_done = sem("p4_idx")
        gathered = sem("p4_gathered")
        var_s = sem("p4_var")
        rstd_s = sem("p4_rstd")
        pooled_s = sem("p4_pooled")
        pT_s = sem("p4_pT")
        pTc_s = sem("p4_pTc")
        b1T_s = sem("p4_b1T")
        l1_s = sem("p4_l1")
        pre_s = sem("p4_pre")
        gelu_s = sem("p4_gelu")
        l2_s = sem("p4_l2")
        oTc_s = sem("p4_oTc")
        oe_s = sem("p4_oe")
        diag_s = sem("p4_diag")
        ibc_s = sem("p4_ibc")
        sel_s = sem("p4_sel")
        add_s = sem("p4_add")
        scat_i = sem("p4_scat_i")
        final_s = sem("p4_final")
        scattered = sem("p4_scattered")
        block = stack.enter_context(nc.Block())
        GR = E // EG

        @block.sync
        def _(sp):
            sp.dma_start(b1[:], weight1[:, C, :]).then_inc(b_in, 16)
            sp.dma_start(b2[:], weight2[:, H, :]).then_inc(b_in, 16)

            def load1(g, s):
                sp.dma_start(w1[:, s], weight1[bass.ds(g * EG, EG), 0:C, :].rearrange("e d h -> d e h")
                             ).then_inc(w1_in[s], 16)

            def load2(g, s):
                for e in range(EG):
                    sp.dma_start(w2[:, s, e], weight2[bass.ds(g * EG + e, 1), 0:H, :].rearrange(
                        "e (c p) o -> p (e c) o", p=P)).then_inc(w2_in[s], 16)

            for s in range(SL):
                load1(s, s)
            sp.wait_ge(based, 1)
            for dst, src in ((mv, cand_v), (mi, cand_i)):
                for h in range(2):
                    sp.dma_start(dst[:, h], src[h * E:(h + 1) * E]).then_inc(merged, 16)
            for h in range(2):
                sp.dma_start(ms[:, h], exp_sum[h * E:(h + 1) * E]).then_inc(merged, 16)
            for s in range(SL):
                load2(s, s)
            for g in range(SL, GR):
                sp.wait_ge(l1_s, g - SL + 1)
                load1(g, g % SL)
            for g in range(SL, GR):
                sp.wait_ge(l2_s, g - SL + 1)
                load2(g, g % SL)

        @block.gpsimd
        def _(pool):
            for h in range(2):
                pool.iota(base[h * E:(h + 1) * E], pattern=[[GT, NG], [0, K]], base=h * HALF * N,
                          channel_multiplier=0, allow_small_or_imprecise_dtypes=True)
            pool.iota(place[:], pattern=[[1, NC2]], base=0, channel_multiplier=0,
                      allow_small_or_imprecise_dtypes=True)
            pool.memset(half[:], -0.5)
            pool.memset(ones[:], 1.0).then_inc(pool_s, 1)
            pool.wait_ge(pool_s, 1)
            pool.affine_select(out=lower[:], in_=ones[:], compare_op=ALU.is_gt, fill=0.0, base=0,
                               pattern=[[-1, E]], channel_multiplier=1).then_inc(pool_s, 1)
            pool.wait_ge(idx_s_done, 1)
            for k in range(K):
                pool.indirect_dma_start(out=xg[:, k, :], out_offset=None, in_=out_tokens,
                                        in_offset=bass.IndirectOffsetOnAxis(ap=idx_u[:, k:k + 1], axis=0)
                                        ).then_inc(gathered, 16)
            pool.wait_ge(var_s, 1)
            pool.tensor_tensor(rstd[:], var_e[:], half[:], ALU.pow).then_inc(rstd_s, 1)
            pool.wait_ge(scat_i, 1)
            pool.wait_ge(final_s, 1)
            for k in range(K):
                if k:
                    pool.wait_ge(scattered, 16 * k)
                pool.indirect_dma_start(out=out_tokens,
                                        out_offset=bass.IndirectOffsetOnAxis(ap=idx_su[:, k:k + 1], axis=0),
                                        in_=final[:, k, :], in_offset=None,
                                        bounds_check=TOKENS - 1, oob_is_err=False).then_inc(scattered, 16)
            pool.wait_ge(scattered, 16 * K)

        @block.vector
        def _(dve):
            count = [0]

            def link(ins):
                count[0] += 1
                ins.then_inc(v, 1)
                dve.wait_ge(v, count[0])

            dve.wait_ge(pool_s, 2)
            dve.tensor_tensor(cand_i[:], cand_i[:], base[:], ALU.add).then_inc(based, 1)
            dve.wait_ge(merged, 16 * 6)
            mvf = mv[:].rearrange("e h g k -> e (h g k)")
            mif = mi[:].rearrange("e h g k -> e (h g k)")
            link(dve.max(v8[:], mvf))
            link(dve.max_index(p8[:], v8[:], mvf))
            dve.tensor_scalar(negm[:], v8[:, 0:1], -1.0, None, ALU.mult).then_inc(max_s, 1)
            link(dve.tensor_copy(p8f[:], p8[:]))
            for k in range(K):
                link(dve.scalar_tensor_tensor(junk[:], place[:], p8f[:, k:k + 1], mif, ALU.is_equal, ALU.mult,
                                              accum_out=idx[:, k:k + 1]))
            dve.tensor_copy(idx_u[:], idx[:]).then_inc(idx_s_done, 1)
            dve.wait_ge(exp_s, 2)
            link(dve.tensor_tensor(eg[:], eg[:], ms[:].rearrange("e h g -> e (h g)"), ALU.mult))
            link(dve.reduce_sum(zsum[:], eg[:], axis=AX.X))
            link(dve.reciprocal(zrec[:], zsum[:]))
            link(dve.tensor_scalar(topv[:], topv[:], zrec[:], None, ALU.mult))
            for k in range(K):
                last = dve.tensor_scalar(diag[:, k, :], ident[0:E, 0:E], idx[:, k:k + 1], None, ALU.mult)
            last.then_inc(diag_s, 1)
            dve.wait_ge(ibc_s, 1)
            link(dve.tensor_copy(idx_bc[:], ps_i[:].rearrange("e (k a) -> e k a", k=K)))
            for k in range(K):
                if k == 0:
                    link(dve.tensor_scalar(sel[:, 0], idx_bc[:], idx[:, k:k + 1], topv[:, k:k + 1],
                                           ALU.is_equal, ALU.mult))
                else:
                    link(dve.tensor_scalar(sel_t[:], idx_bc[:], idx[:, k:k + 1], topv[:, k:k + 1],
                                           ALU.is_equal, ALU.mult))
                    link(dve.tensor_tensor(sel[:, k % 2], sel[:, (k - 1) % 2], sel_t[:], ALU.add))
            for k in range(K):
                link(dve.scalar_tensor_tensor(junk[:, 0:E], idx_bc[:, k, :], idx[:, k:k + 1], lower[:],
                                              ALU.is_equal, ALU.mult, accum_out=dup[:, k:k + 1]))
            link(dve.scalar_tensor_tensor(idx_s[:], dup[:], float(TOKENS), idx[:], ALU.mult, ALU.add))
            dve.tensor_copy(idx_su[:], idx_s[:]).then_inc(scat_i, 1)
            dve.wait_ge(gathered, 16 * K)
            for k in range(K):
                last = dve.bn_stats(st[:, k, :], xg[:, k, :])
            link(last)
            for k in range(K):
                last = dve.bn_aggr(mean_var[:, k, :], st[:, k, :])
            link(last)
            dve.tensor_scalar(var_e[:], mean_var[:, :, 1], LN_EPS, None, ALU.add).then_inc(var_s, 1)
            dve.wait_ge(rstd_s, 1)
            link(dve.scalar_tensor_tensor(nbias[:], mean_var[:, :, 0], -1.0, rstd[:], ALU.mult, ALU.mult))
            for k in range(K):
                last = dve.tensor_scalar(xgn[:, k, :], xg[:, k, :], rstd[:, k:k + 1], nbias[:, k:k + 1],
                                         ALU.mult, ALU.add)
            link(last)
            for k in range(K):
                if k == 0:
                    ins = dve.tensor_scalar(pooled[:], xgn[:, k, :], topv[:, k:k + 1], None, ALU.mult)
                else:
                    ins = dve.scalar_tensor_tensor(pooled[:], xgn[:, k, :], topv[:, k:k + 1], pooled[:],
                                                   ALU.mult, ALU.add)
                if k < K - 1:
                    link(ins)
            ins.then_inc(pooled_s, 1)
            dve.wait_ge(pT_s, 1)
            dve.tensor_copy(pooledT[:], ps_p[:]).then_inc(pTc_s, 1)
            dve.wait_ge(b1T_s, 1)
            link(dve.tensor_copy(b1T[:], ps_b[:].rearrange("p (c e) -> p c e", c=HC)))
            dve.wait_ge(l1_s, GR)
            dve.tensor_tensor(h_pre[:], ps_h[:].rearrange("p (c e) -> p c e", c=HC), b1T[:], ALU.add).then_inc(pre_s, 1)
            dve.wait_ge(l2_s, GR)
            dve.tensor_copy(oT[:], ps_oT[:]).then_inc(oTc_s, 1)
            dve.wait_ge(oe_s, 1)
            dve.tensor_tensor(out_e[:], ps_oe[:], b2[:], ALU.add).then_inc(sel_s, 1)
            dve.wait_ge(add_s, 1)
            for n in range(2):
                last = dve.tensor_tensor(final[:, 4 * n:4 * n + 4, :], ps_r[n][:].rearrange("e (k c) -> e k c", k=4),
                                         xg[:, 4 * n:4 * n + 4, :], ALU.add)
            last.then_inc(final_s, 1)

        @block.scalar
        def _(act):
            act.wait_ge(max_s, 1)
            act.activation(eg[:], mv[:].rearrange("e h g k -> e (h g) k")[:, :, 0], ACT.Exp,
                           bias=negm[:]).then_inc(exp_s, 1)
            act.activation(topv[:], v8[:], ACT.Exp, bias=negm[:]).then_inc(exp_s, 1)
            act.wait_ge(pre_s, 1)
            act.activation(hT[:], h_pre[:], ACT.Gelu).then_inc(gelu_s, 1)

        @block.tensor
        def _(pe):
            pe.wait_ge(diag_s, 1)
            pe.matmul(ps_i[:], ones[:], diag[:].rearrange("e k a -> e (k a)"), start=True, stop=True).then_inc(ibc_s, 1)
            pe.wait_ge(b_in, 32)
            for c in range(HC):
                last = pe.transpose(ps_b[:, c * E:(c + 1) * E], b1[:, c * P:(c + 1) * P], ident[0:E, 0:E])
            last.then_inc(b1T_s, 1)
            pe.wait_ge(pooled_s, 1)
            pe.transpose(ps_p[:], pooled[:], ident[0:E, 0:E]).then_inc(pT_s, 1)
            pe.wait_ge(pTc_s, 1)
            with pe.Fori(0, GR // SL) as gg:
                for s in range(SL):
                    pe.wait_ge(w1_in[s], (gg + 1) * 16)
                    for x in range(EG):
                        e = gg * (SL * EG) + s * EG + x
                        for c in range(HC):
                            last = pe.matmul(ps_h[:, bass.ds(e + c * E, 1)], w1[:, s, x, c * P:(c + 1) * P],
                                             pooledT[:, bass.ds(e, 1)], start=True, stop=True)
                    last.then_inc(l1_s, 1)
            pe.wait_ge(gelu_s, 1)
            hTf = hT[:].rearrange("p c e -> p (c e)")
            with pe.Fori(0, GR // SL) as gg:
                for s in range(SL):
                    pe.wait_ge(w2_in[s], (gg + 1) * 16 * EG)
                    for x in range(EG):
                        e = gg * (SL * EG) + s * EG + x
                        for c in range(HC):
                            last = pe.matmul(ps_oT[:, bass.ds(e, 1)], w2[:, s, x, c, :],
                                             hTf[:, bass.ds(e + c * E, 1)], start=(c == 0), stop=(c == HC - 1))
                    last.then_inc(l2_s, 1)
            pe.wait_ge(oTc_s, 1)
            pe.transpose(ps_oe[:], oT[:], ident[:]).then_inc(oe_s, 1)
            pe.wait_ge(sel_s, 1)
            for k in range(K):
                last = pe.matmul(ps_r[k // 4][:, k % 4 * C:(k % 4 + 1) * C], sel[:, (K - 1) % 2, k, :], out_e[:],
                                 start=True, stop=True)
            last.then_inc(add_s, 1)


_INS = ['x', 'L0_conv_mask', 'L0_conv_ln_g', 'L0_conv_ln_b', 'L0_conv_Wl', 'L0_conv_bl', 'L0_conv_Wr',
        'L0_conv_br', 'L0_conv_Wgl', 'L0_conv_bgl', 'L0_conv_Wgr', 'L0_conv_bgr', 'L0_conv_cg', 'L0_conv_cb',
        'L0_conv_Wo', 'L0_conv_bo', 'L0_conv_Wg', 'L0_conv_bg', 'L0_ffn_gate_w', 'L0_ffn_gate_b',
        'L0_ffn_weight1', 'L0_ffn_weight2']
_OUTS = [((1, N, N, C), 'float32')]


def kernel(**inputs):
    import numpy as _np
    import concourse.bacc as _bacc
    from concourse import mybir as _mybir
    from concourse.bass_utils import run_bass_kernel_spmd as _run

    nc = _bacc.Bacc("TRN2", target_bir_lowering=False, num_devices=1)
    arrays, args = {}, []
    for name in _INS:
        a = _np.ascontiguousarray(inputs[name])
        arrays[f"in_{name}_dram"] = a
        args.append(nc.dram_tensor(f"in_{name}_dram", a.shape, _mybir.dt.from_np(a.dtype), kind="ExternalInput").ap())
    for i, (shape, dtype) in enumerate(_OUTS):
        args.append(nc.dram_tensor(f"out_{i}_dram", shape, _mybir.dt.from_np(_np.dtype(dtype)),
                                   kind="ExternalOutput").ap())
    mk_metaformer(nc, *args)
    r = _run(nc, [arrays], core_ids=[0])
    return r.results[0]["out_0_dram"]
```

```python
import concourse.bass as bass
from concourse import mybir
from contextlib import ExitStack

F32 = mybir.dt.float32
F32R = mybir.dt.float32r
U32 = mybir.dt.uint32
ALU = mybir.AluOpType
ACT = mybir.ActivationFunctionType
AX = mybir.AxisListType

N = 384
C = 128
E, H, O, K = 64, 512, 128, 8
P = 128
T = N // P
TOKENS = N * N
HC = H // P

CW = 8
CG = C // CW
IB = 16
NB = N // IB

CONV_EPS1, CONV_EPS2 = 1e-6, 1e-5
LN_EPS = 1e-5

HALF = N // 2
GROUP = 4
GT = GROUP * N
NG = HALF // GROUP


def after(eng, sem, count):
    if isinstance(count, int) and count <= 0:
        return
    eng.wait_ge(sem, count)


class Step:

    def __init__(self, q, k, body, count):
        self.q, self.k, self.body, self.count = q, k, body, count

    def __add__(self, more):
        return Step(self.q + (self.k + more) // self.body, (self.k + more) % self.body, self.body, self.count)

    def __sub__(self, less):
        return self + -less

    def number(self, more=0, each=1):
        return self.q * (self.body * each) + (self.k * each + more)

    def group(self, size, more=0):
        return self.q * (self.body // size) + (self.k // size + more)

    def exists(self):
        return not isinstance(self.q, int) or 0 <= self.number() < self.count


def steps(eng, step, count, body, lead, first=1):
    for n in range(-lead, first * body):
        step(Step(n // body, n % body, body, count))
    whole = count // body
    with eng.Fori(first, whole - 1) as q:
        for k in range(body):
            step(Step(q, k, body, count))
    for n in range((whole - 1) * body, (whole + 1) * body):
        step(Step(n // body, n % body, body, count))


def mk_metaformer(nc, x, mask, ln_g, ln_b, Wl, bl, Wr, br, Wgl, bgl, Wgr, bgr, cg, cb, Wo, bo, Wg, bg,
                  gate_w, gate_b, weight1, weight2, out):
    sides_d = nc.dram_tensor("sides_scratch", [2, CG, T, P, NB, IB * CW], F32).ap()
    prod_d = nc.dram_tensor("product_scratch", [C, N, N], F32).ap()

    x_rows = x.rearrange("a i (p t) c -> (a i) p (t c)", t=T)
    out_rows = out.rearrange("a i (p t) c -> (a i) p (t c)", t=T)
    out_tokens = out.rearrange("a i j c -> (a i j) c")

    def tensors(stack):
        def sb(name, shape, dt=F32):
            return stack.enter_context(nc.sbuf_tensor(name, shape, dt))

        def pb(name, shape, dt=F32):
            return stack.enter_context(nc.psum_tensor(name, shape, dt))

        def sem(name):
            return stack.enter_context(nc.semaphore(name))
        return sb, pb, sem

    with ExitStack() as keep:
        sb, _, _ = tensors(keep)
        ident = sb("ident", [P, P])
        wg_c = sb("wg_c", [C, C])
        wo_c = sb("wo_c", [C, C])
        bo_bc = sb("bo_bc", [P, C])
        gate_wT = sb("gate_wT", [C, E])
        gate_b2 = sb("gate_b2", [P, 1])
        x_scale = sb("x_scale", [P, N, T])
        x_shift = sb("x_shift", [P, N, T])
        with ExitStack() as early:
            sb, _, _ = tensors(early)
            w_hi = sb("w_hi", [C, 4 * C], F32R)
            w_lo = sb("w_lo", [C, 4 * C], F32R)
            mask_T = sb("mask_T", [P, T, N])
            prepare(nc, tensors, ident, w_hi, w_lo, wg_c, wo_c, bo_bc, gate_wT, gate_b2, mask_T,
                    mask, ln_g, ln_b, (Wl, Wr, Wgl, Wgr, Wg), (bl, br, bgl, bgr, bg), cg, cb, Wo, bo,
                    gate_w, gate_b)
            project(nc, tensors, x_rows, sides_d, ident, w_hi, w_lo, mask_T, x_scale, x_shift)
        multiply(nc, tensors, sides_d, prod_d)
        sb, _, _ = tensors(keep)
        cand_v = sb("cand_v", [P, NG, K])
        cand_i = sb("cand_i", [P, NG, K])
        exp_sum = sb("exp_sum", [P, NG])
        finish_rows(nc, tensors, x_rows, out_rows, prod_d, ident, wg_c, wo_c, bo_bc, gate_wT, gate_b2,
                    x_scale, x_shift, cand_v, cand_i, exp_sum)
        experts(nc, tensors, out_tokens, ident, cand_v, cand_i, exp_sum, weight1, weight2)


def prepare(nc, tensors, ident, w_hi, w_lo, wg_c, wo_c, bo_bc, gate_wT, gate_b2, mask_T,
            mask, ln_g, ln_b, weights, biases, cg, cb, Wo, bo, gate_w, gate_b):
    NW = 5 * C
    column = "(c o) -> c o"
    with ExitStack() as stack:
        sb, pb, sem = tensors(stack)
        w_all = sb("w_all", [C, NW])
        wo_raw = sb("wo_raw", [C, C])
        gw_raw = sb("gw_raw", [E, C])
        mask_raw = sb("mask_raw", [P, T, N])
        g_col = sb("g_col", [C, 1])
        b_col = sb("b_col", [C, 1])
        cg_col = sb("cg_col", [C, 1])
        cb_col = sb("cb_col", [C, 1])
        b_row = sb("b_row", [1, NW])
        bo_row = sb("bo_row", [1, C])
        one_row = sb("one_row", [1, P])
        ones = sb("ones", [P, P])
        minus = sb("minus", [P, P])
        b_wide = sb("b_wide", [C, P])
        cb_wide = sb("cb_wide", [C, P])
        wp = sb("wp", [C, NW])
        wop = sb("wop", [C, C])
        wc = sb("wc", [C, NW])
        ps_a = pb("ps_a", [P, 4 * C])
        ps_b = pb("ps_b", [P, C])
        ps_o = pb("ps_o", [P, C])
        ps_bo = pb("ps_bo", [P, C])
        ps_g = pb("ps_g", [C, E])
        ps_m = [pb(f"ps_m{n}", [P, N]) for n in range(2)]
        loaded = sem("prep_loaded")
        ident_done = sem("prep_ident")
        vec = sem("prep_vec")
        folded = sem("prep_folded")
        pe_done = sem("prep_pe")
        mask_pe = sem("prep_mask_pe")
        mask_cp = sem("prep_mask_cp")
        LOADS = 2 * len(weights) + 10
        block = stack.enter_context(nc.Block())

        @block.sync
        def _(sp):
            n = 0
            for at, w in enumerate(weights):
                sp.dma_start(w_all[:, at * C:(at + 1) * C], w).then_inc(loaded, 16)
                sp.dma_start(b_row[0:1, at * C:(at + 1) * C],
                             biases[at].rearrange("(o c) -> o c", o=1)).then_inc(loaded, 16)
                n += 2
            for dst, src in ((wo_raw[:], Wo), (gw_raw[:], gate_w),
                             (mask_raw[:], mask.rearrange("a (r p) j -> p (a r) j", p=P)),
                             (bo_row[:], bo.rearrange("(o c) -> o c", o=1)),
                             (g_col[:], ln_g.rearrange(column, o=1)), (b_col[:], ln_b.rearrange(column, o=1)),
                             (cg_col[:], cg.rearrange(column, o=1)), (cb_col[:], cb.rearrange(column, o=1)),
                             (gate_b2[0:E, :], gate_b.rearrange(column, o=1)),
                             (gate_b2[E:2 * E, :], gate_b.rearrange(column, o=1))):
                sp.dma_start(dst, src).then_inc(loaded, 16)
                n += 1
            assert n == LOADS

        @block.gpsimd
        def _(pool):
            pool.memset(ident[:], 0.0).then_inc(ident_done, 1)
            pool.wait_ge(ident_done, 1)
            pool.affine_select(out=ident[:], in_=ident[:], compare_op=ALU.not_equal, fill=1.0,
                               base=0, pattern=[[-1, P]], channel_multiplier=1).then_inc(ident_done, 1)

        @block.vector
        def _(dve):
            dve.memset(ones[:], 1.0)
            dve.memset(minus[:], -1.0)
            dve.memset(one_row[:], 1.0).then_inc(vec, 1)
            dve.wait_ge(vec, 1)
            dve.wait_ge(loaded, 16 * LOADS)
            dve.tensor_scalar(b_wide[:], ones[:], b_col[:], None, ALU.mult)
            dve.tensor_scalar(cb_wide[:], ones[:], cb_col[:], None, ALU.mult)
            dve.tensor_scalar(wp[:], w_all[:], g_col[:], None, ALU.mult)
            dve.tensor_scalar(wop[:], wo_raw[:], cg_col[:], None, ALU.mult).then_inc(folded, 1)
            dve.wait_ge(pe_done, 1)
            dve.scalar_tensor_tensor(wc[:, 0:4 * C], ps_a[:], 1.0 / C, wp[:, 0:4 * C], ALU.mult, ALU.add)
            dve.scalar_tensor_tensor(wg_c[:], ps_b[:], 1.0 / C, wp[:, 4 * C:], ALU.mult, ALU.add)
            dve.scalar_tensor_tensor(wo_c[:], ps_o[:], 1.0 / C, wop[:], ALU.mult, ALU.add)
            dve.tensor_copy(bo_bc[:], ps_bo[:])
            dve.tensor_copy(gate_wT[:], ps_g[:]).then_inc(vec, 1)
            dve.wait_ge(vec, 2)
            dve.tensor_copy(w_hi[:], wc[:, 0:4 * C]).then_inc(vec, 1)
            dve.wait_ge(vec, 3)
            dve.tensor_tensor(w_lo[:], wc[:, 0:4 * C], w_hi[:].bitcast(F32), ALU.subtract)
            for t in range(T):
                dve.wait_ge(mask_pe, t + 1)
                dve.tensor_copy(mask_T[:, t, :], ps_m[t % 2][:]).then_inc(mask_cp, 1)

        @block.tensor
        def _(pe):
            pe.wait_ge(ident_done, 2)
            pe.wait_ge(folded, 1)
            pe.matmul(ps_a[:], minus[:], wp[:, 0:4 * C], start=True, stop=False)
            pe.matmul(ps_a[:], b_wide[:], w_all[:, 0:4 * C], start=False, stop=False)
            pe.matmul(ps_a[:], one_row[:], b_row[0:1, 0:4 * C], start=False, stop=True)
            pe.matmul(ps_b[:], minus[:], wp[:, 4 * C:], start=True, stop=False)
            pe.matmul(ps_b[:], b_wide[:], w_all[:, 4 * C:], start=False, stop=False)
            pe.matmul(ps_b[:], one_row[:], b_row[0:1, 4 * C:], start=False, stop=True)
            pe.matmul(ps_o[:], minus[:], wop[:], start=True, stop=True)
            pe.matmul(ps_bo[:], cb_wide[:], wo_raw[:], start=True, stop=False)
            pe.matmul(ps_bo[:], one_row[:], bo_row[:], start=False, stop=True)
            pe.transpose(ps_g[:], gw_raw[:], ident[0:E, 0:E]).then_inc(pe_done, 1)
            for t in range(T):
                if t >= 2:
                    pe.wait_ge(mask_cp, t - 1)
                for r in range(T):
                    last = pe.transpose(ps_m[t % 2][:, r * P:(r + 1) * P], mask_raw[:, r, t::T], ident[:])
                last.then_inc(mask_pe, 1)


def norm_scale(pool, st, s, gain, eps, minus_half, done):
    pool.tensor_tensor(s[:, 0], st[:, :, 1], st[:, :, 4], ALU.add)
    pool.tensor_tensor(s[:, 1], st[:, :, 1], st[:, :, 4], ALU.subtract)
    pool.tensor_tensor(s[:, 2], st[:, :, 2], st[:, :, 5], ALU.add)
    pool.drain()
    pool.tensor_scalar(s[:, 4], s[:, 0], 0.5, 0.0, ALU.mult, ALU.add)
    pool.tensor_scalar(s[:, 1], s[:, 1], (gain ** 0.5) / 2, 0.0, ALU.mult, ALU.add)
    pool.tensor_scalar(s[:, 2], s[:, 2], gain / C, eps, ALU.mult, ALU.add)
    pool.drain()
    pool.tensor_tensor(s[:, 1], s[:, 1], s[:, 1], ALU.mult)
    pool.drain()
    pool.tensor_tensor(s[:, 2], s[:, 2], s[:, 1], ALU.add)
    pool.drain()
    last = pool.tensor_tensor(s[:, 3], s[:, 2], minus_half[:], ALU.pow)
    if done is not None:
        last.then_inc(done, 1)
    pool.drain()


def project(nc, tensors, x_rows, sides_d, ident, w_hi, w_lo, mask_T, x_scale, x_shift):
    U = IB
    AHEAD_STATS, AHEAD_NORM, AHEAD_T, AHEAD_SPLIT = 8, 3, 2, 1
    with ExitStack() as stack:
        sb, pb, sem = tensors(stack)
        xin = sb("xin", [P, U, T * C])
        st = sb("st", [P, U, T, 6])
        small = sb("small", [P, U // 2, 6, 2 * T])
        minus_half = sb("minus_half", [P, 2 * T])
        xn = sb("xn", [P, U // 2, T, C])
        xT_hi = [sb(f"xT_hi{n}", [C, N], F32R) for n in range(2)]
        xT_lo = [sb(f"xT_lo{n}", [C, N], F32R) for n in range(2)]
        gates = sb("gates", [P, 2 * T, 2 * C])
        stage = sb("stage", [P, 2, T, 2, CG, IB, CW])
        ps_x = [pb(f"ps_x{n}", [C, N]) for n in range(2)]
        ps_w = [pb(f"ps_w{n}", [P, 4 * C]) for n in range(2 * T)]
        x_loaded = [sem(f"x_loaded{n}") for n in range(U // 2)]
        half_set = sem("half_set")
        stats_done = sem("p1_stats")
        scale_done = sem("p1_scale")
        xn_done = sem("p1_xn")
        xT_done = sem("p1_xT")
        hi_done = sem("p1_hi")
        lo_done = sem("p1_lo")
        proj_done = sem("p1_proj")
        sig_done = sem("p1_sig")
        gated = sem("p1_gated")
        stored = [sem(f"p1_stored{n}") for n in range(2)]
        block = stack.enter_context(nc.Block())

        @block.sync
        def _(sp):
            def load(pair, k):
                after(sp, xn_done, pair * 2 + (2 - U))
                sp.dma_start(xin[:, 2 * k:2 * k + 2, :],
                             x_rows[bass.ds(pair * 2, 2)].rearrange("r p n -> p r n")).then_inc(x_loaded[k], 16)

            PAIRS = IB // 2
            AHEAD = 6

            def store(b, buf, piece):
                t, side = divmod(piece, 2)
                if piece == 0:
                    sp.wait_ge(gated, (b + 1) * IB * T)
                sp.dma_start(sides_d[side, :, t, :, bass.ds(b, 1), :].rearrange("g p b n -> p g (b n)"),
                             stage[:, buf, t, side].rearrange("p g i c -> p g (i c)")).then_inc(stored[buf], 16)

            def block_of_rows(b, buf):
                for j in range(PAIRS):
                    if not isinstance(b, int) or b * PAIRS + j + AHEAD < N // 2:
                        load(b * PAIRS + j + AHEAD, (j + AHEAD) % PAIRS)
                    if j < 2 * T and (not isinstance(b, int) or b > 0):
                        store(b - 1, 1 - buf, j)

            for pair in range(AHEAD):
                load(pair, pair)
            for b in range(2):
                block_of_rows(b, b)
            with sp.Fori(1, NB // 2 - 1) as bb:
                for buf in range(2):
                    block_of_rows(bb * 2 + buf, buf)
            for b in range(NB - 2, NB):
                block_of_rows(b, b % 2)
            for piece in range(2 * T):
                store(NB - 1, (NB - 1) % 2, piece)
            for buf in range(2):
                sp.wait_ge(stored[buf], 16 * 2 * T * (NB // 2))

        @block.vector
        def _(dve):
            dve.memset(minus_half[:], -0.5).then_inc(half_set, 1)

            def stats(row):
                k = row.k
                dve.wait_ge(x_loaded[k // 2], row.group(U, 1) * 16)
                after(dve, scale_done, row.group(2, 1 - U // 2))
                for t in range(T):
                    last = dve.bn_stats(st[:, k, t, :], xin[:, k, t * C:(t + 1) * C])
                last.then_inc(stats_done, 1)

            def split(row):
                dve.wait_ge(hi_done, row.number(1))
                after(dve, proj_done, row.number(-T, T))
                par = row.k % 2
                dve.tensor_tensor(xT_lo[par][:], ps_x[par][:], xT_hi[par][:].bitcast(F32),
                                  ALU.subtract).then_inc(lo_done, 1)

            def gate(row):
                k, q = row.k, row.q
                buf, ii = (q // (IB // U)) % 2, (q % (IB // U)) * U + k
                if k == 0:
                    after(dve, stored[0], q // (2 * IB // U) * (16 * 2 * T))
                    after(dve, stored[1], (q - IB // U) // (2 * IB // U) * (16 * 2 * T))
                for t in range(T):
                    tile = k % 2 * T + t
                    dve.wait_ge(sig_done, row.number(t + 1, T))
                    dve.scalar_tensor_tensor(
                        stage[:, bass.ds(buf, 1), t, :, :, bass.ds(ii, 1), :].rearrange(
                            "p b s g i c -> p (b s g) (i c)"),
                        ps_w[tile][:, 0:2 * C].rearrange("p (g c) -> p g c", c=CW),
                        mask_T[:, t, bass.ds(row.number(), 1)],
                        gates[:, tile, :].rearrange("p (g c) -> p g c", c=CW),
                        ALU.mult, ALU.mult).then_inc(gated, 1)

            def step(row):
                if (row + AHEAD_SPLIT).exists():
                    split(row + AHEAD_SPLIT)
                if row.exists():
                    gate(row)
                if (row + AHEAD_STATS).exists():
                    stats(row + AHEAD_STATS)

            steps(dve, step, N, U, AHEAD_STATS, first=2)

        @block.gpsimd
        def _(pool):
            pool.wait_ge(half_set, 1)

            def scales(row):
                k = row.k
                s = small[:, k // 2]
                pool.wait_ge(stats_done, row.number(2))
                after(pool, xn_done, row.number(2 - U))
                norm_scale(pool, st[:, k:k + 2].rearrange("p r t s -> p (r t) s"), s,
                           1.0 + CONV_EPS2, CONV_EPS1 * CONV_EPS2, minus_half, None)
                pool.tensor_tensor(s[:, 4], s[:, 4], s[:, 3], ALU.mult)
                pool.drain()
                pool.tensor_scalar(s[:, 5], s[:, 4], -1.0, 1.0, ALU.mult, ALU.add).then_inc(scale_done, 1)
                pool.drain()
                pool.tensor_copy(x_scale[:, bass.ds(row.number(), 2), :], s[:, 3].rearrange("p (r t) -> p r t", t=T))
                pool.tensor_copy(x_shift[:, bass.ds(row.number(), 2), :], s[:, 5].rearrange("p (r t) -> p r t", t=T))

            def step(row):
                if (row + AHEAD_STATS).exists() and row.k % 2 == 0:
                    scales(row + AHEAD_STATS)

            steps(pool, step, N, U, AHEAD_STATS)

        @block.tensor
        def _(pe):
            def transposes(row):
                k = row.k
                pe.wait_ge(xn_done, row.number(1))
                after(pe, lo_done, row.number(-1))
                for t in range(T):
                    last = pe.transpose(ps_x[k % 2][:, t * P:(t + 1) * P], xn[:, k % (U // 2), t, :], ident[:])
                last.then_inc(xT_done, 1)

            def projections(row):
                k = row.k
                hi, lo = xT_hi[k % 2], xT_lo[k % 2]
                pe.wait_ge(lo_done, row.number(1))
                for t in range(T):
                    dst = ps_w[k % 2 * T + t]
                    at = slice(t * P, (t + 1) * P)
                    after(pe, gated, row.number(t + 1 - 2 * T, T))
                    pe.matmul(dst[:], hi[:, at], w_hi[:], start=True, stop=False)
                    pe.matmul(dst[:], hi[:, at], w_lo[:], start=False, stop=False)
                    pe.matmul(dst[:], lo[:, at], w_hi[:], start=False, stop=True).then_inc(proj_done, 1)

            def step(row):
                if (row + AHEAD_T).exists():
                    transposes(row + AHEAD_T)
                if row.exists():
                    projections(row)

            steps(pe, step, N, U, AHEAD_T)

        @block.scalar
        def _(act):
            def normalise(row):
                k = row.k
                act.wait_ge(scale_done, row.group(2, 1))
                after(act, xT_done, row.number(1 - U // 2))
                s = small[:, k // 2]
                for t in range(T):
                    at = k % 2 * T + t
                    last = act.activation(xn[:, k % (U // 2), t, :], xin[:, k, t * C:(t + 1) * C], ACT.Identity,
                                          bias=s[:, 5, at:at + 1], scale=s[:, 3, at:at + 1])
                last.then_inc(xn_done, 1)

            def upper(row):
                k = row.k
                act.wait_ge(xT_done, row.number(1))
                after(act, proj_done, row.number(-T, T))
                act.activation(xT_hi[k % 2][:], ps_x[k % 2][:], ACT.Copy).then_inc(hi_done, 1)

            def sigmoids(row):
                for t in range(T):
                    tile = row.k % 2 * T + t
                    act.wait_ge(proj_done, row.number(t + 1, T))
                    act.activation(gates[:, tile, :], ps_w[tile][:, 2 * C:4 * C],
                                   ACT.Sigmoid).then_inc(sig_done, 1)

            def step(row):
                if (row + AHEAD_SPLIT).exists():
                    upper(row + AHEAD_SPLIT)
                if (row + AHEAD_NORM).exists():
                    normalise(row + AHEAD_NORM)
                if row.exists():
                    sigmoids(row)

            steps(act, step, N, U, AHEAD_NORM)


def multiply(nc, tensors, sides_d, prod_d):
    RT = N // P
    U = 2
    with ExitStack() as stack:
        sb, pb, sem = tensors(stack)
        raw = sb("raw", [P, 2, 2, T, N, CW])
        hi = [sb(f"hi{n}", [P, 2, T, N], F32R) for n in range(U)]
        lo = [sb(f"lo{n}", [P, 2, T, N], F32R) for n in range(U)]
        prod = sb("prod", [P, U, RT, N])
        ps = [pb(f"ps_p{n}", [P, N]) for n in range(U * RT)]
        loaded = [sem(f"p2_loaded{n}") for n in range(2)]
        hi_done = sem("p2_hi")
        lo_done = sem("p2_lo")
        summed = sem("p2_summed")
        copied_a = sem("p2_copied_a")
        copied_v = sem("p2_copied_v")
        stored = [sem(f"p2_stored{n}") for n in range(U)]
        block = stack.enter_context(nc.Block())

        @block.sync
        def _(sp):
            def load(g, buf):
                for piece in range(2 * T):
                    side, t = divmod(piece, T)
                    after(sp, lo_done, (g - 1) * (2 * CW) + 2 * piece)
                    sp.dma_start(raw[:, buf, side, t].rearrange("p i c -> p (i c)"),
                                 sides_d[side, bass.ds(g, 1), t].rearrange("g p b n -> p (g b n)")
                                 ).then_inc(loaded[buf], 16)

            load(0, 0)
            load(1, 1)
            with sp.Fori(1, CG // 2) as gg:
                for buf in range(2):
                    load(gg * 2 + buf, buf)

        def part(ch, side):
            c = ch.number()
            v = raw[:, bass.ds((c // CW) % 2, 1), side, :, :, bass.ds(c % CW, 1)]
            return v.rearrange("p b t i c -> p (b t) (i c)")

        @block.scalar
        def _(act):
            def upper(ch):
                if ch.k == 0:
                    g = ch.number() // CW
                    act.wait_ge(loaded[0], (g + 2) // 2 * (16 * 2 * T))
                    after(act, loaded[1], (g + 1) // 2 * (16 * 2 * T))
                after(act, summed, ch.number(-RT, RT))
                for side in range(2):
                    act.activation(hi[ch.k][:, side], part(ch, side), ACT.Copy).then_inc(hi_done, 1)

            def copy(ch):
                act.wait_ge(summed, ch.number(1, RT))
                after(act, stored[ch.k], ch.group(U) * 16)
                act.activation(prod[:, ch.k, 0, :], ps[ch.k * RT][:], ACT.Copy).then_inc(copied_a, 1)

            def store(ch):
                act.wait_ge(copied_a, ch.number(1))
                act.wait_ge(copied_v, ch.number(1))
                act.dma_start(prod_d[bass.ds(ch.number(), 1)].rearrange("c (r p) j -> p (c r) j", p=P),
                              prod[:, ch.k]).then_inc(stored[ch.k], 16)

            def step(ch):
                if (ch + 1).exists():
                    upper(ch + 1)
                if (ch - 1).exists():
                    store(ch - 1)
                if ch.exists():
                    copy(ch)

            steps(act, step, C, U, 1)
            for k in range(U):
                act.wait_ge(stored[k], 16 * (C // U))

        @block.vector
        def _(dve):
            def lower(ch):
                for side in range(2):
                    dve.wait_ge(hi_done, ch.number(side + 1, 2))
                    if side == 0:
                        after(dve, summed, ch.number(-RT, RT))
                    dve.tensor_tensor(lo[ch.k][:, side], part(ch, side), hi[ch.k][:, side].bitcast(F32),
                                      ALU.subtract).then_inc(lo_done, 1)

            def copy(ch):
                for r in range(1, RT):
                    dve.wait_ge(summed, ch.number(r + 1, RT))
                    if r == 1:
                        after(dve, stored[ch.k], ch.group(U) * 16)
                    last = dve.tensor_copy(prod[:, ch.k, r, :], ps[ch.k * RT + r][:])
                last.then_inc(copied_v, 1)

            def step(ch):
                if (ch + 1).exists():
                    lower(ch + 1)
                if ch.exists():
                    copy(ch)

            steps(dve, step, C, U, 1)

        @block.tensor
        def _(pe):
            def step(ch):
                if not ch.exists():
                    return
                k = ch.k
                pe.wait_ge(lo_done, ch.number(2, 2))
                after(pe, copied_a, ch.number(1 - U))
                after(pe, copied_v, ch.number(1 - U))
                for r in range(RT):
                    at = slice(r * P, (r + 1) * P)
                    for t in range(T):
                        pe.matmul(ps[k * RT + r][:], hi[k][:, 0, t, at], hi[k][:, 1, t, :],
                                  start=(t == 0), stop=False)
                        pe.matmul(ps[k * RT + r][:], hi[k][:, 0, t, at], lo[k][:, 1, t, :],
                                  start=False, stop=False)
                        last = pe.matmul(ps[k * RT + r][:], lo[k][:, 0, t, at], hi[k][:, 1, t, :],
                                         start=False, stop=(t == T - 1))
                    last.then_inc(summed, 1)

            steps(pe, step, C, U, 0)


def finish_rows(nc, tensors, x_rows, out_rows, prod_d, ident, wg_c, wo_c, bo_bc, gate_wT, gate_b2,
                x_scale, x_shift, cand_v, cand_i, exp_sum):
    U = 2 * GROUP
    LOAD, NORM, TURN, WEIGH = 6, 3, 2, 1
    ADD, RECORD, NORM1, TURN1, LOGITS, SEARCH, EXPS = 1, 2, 3, 4, 5, 6, 7
    x_pairs = x_rows.rearrange("(h n) p f -> n p h f", h=2)
    out_pairs = out_rows.rearrange("(h n) p f -> n p h f", h=2)
    prod_pairs = prod_d.rearrange("c (h n) j -> n c h j", h=2)
    with ExitStack() as stack:
        sb, pb, sem = tensors(stack)
        prodT = [sb(f"prodT{n}", [C, 2, N]) for n in range(U)]
        xin = sb("x3", [P, U, 2, T * C])
        xn = sb("xn3", [P, 2, 2, T, C])
        xnT = [sb(f"xnT{n}", [C, N]) for n in range(4)]
        gates = sb("gates3", [P, 2, 2, T * C])
        branch = sb("branch", [P, 2, 2, T * C])
        x1 = sb("x1", [P, U, 2, T * C])
        st = sb("st3", [P, 2, 2, 2, T, 6])
        small = sb("small3", [P, 4, 5, 4 * T])
        minus_half = sb("minus_half3", [P, 4 * T])
        x1n = sb("x1n", [P, 2, T, C])
        x1T = [sb(f"x1T{n}", [C, N]) for n in range(4)]
        logits = sb("logits", [P, 2, GT])
        top_v = sb("top_v", [P, 2, K])
        top_i = sb("top_i", [P, 2, K], U32)
        neg_max = sb("neg_max", [P, 2])
        exps = sb("exps", [P, GT])
        ps_x = pb("ps3_x", [C, N])
        ps_g = pb("ps3_g", [P, N])
        ps_o = [pb(f"ps3_o{n}", [P, N]) for n in range(2)]
        ps_y = [pb(f"ps3_y{n}", [P, N]) for n in range(2)]
        ps_t = pb("ps3_t", [C, N])
        ps_l = pb("ps3_l", [P, N])
        loaded = [sem(f"p3_loaded{n}") for n in range(U)]
        stored = [sem(f"p3_stored{n}") for n in range(U)]
        half_set = sem("p3_half")
        st_set = sem("p3_st")
        xn_done = sem("p3_xn")
        scales_done = sem("p3_scales")
        x1_done = sem("p3_x1")
        x1n_done = sem("p3_x1n")
        xT_done = sem("p3_xT")
        oT_done = sem("p3_oT")
        g_done = sem("p3_g")
        y_done = sem("p3_y")
        x1T_done = sem("p3_x1T")
        l_done = sem("p3_l")
        xcp_done = sem("p3_xcp")
        gate_done = sem("p3_gate")
        x1cp_done = sem("p3_x1cp")
        log_done = sem("p3_log")
        o_stats = sem("p3_ostats")
        x1_stats = sem("p3_x1stats")
        bias_done = sem("p3_bias")
        gated = sem("p3_gated")
        exp_done = sem("p3_exp")
        top_found = sem("p3_top")
        neg_done = sem("p3_neg")
        place_done = sem("p3_place")
        block = stack.enter_context(nc.Block())

        @block.sync
        def _(sp):
            def load(pair):
                k = pair.k
                after(sp, y_done, pair.number(2 - 2 * U, 2))
                after(sp, x1_done, pair.number(2 - 2 * U, 2))
                n = pair.number()
                sp.dma_start(prodT[k][:], prod_pairs[bass.ds(n, 1)].rearrange("n c h j -> c (n h) j")
                             ).then_inc(loaded[k], 16)
                sp.dma_start(xin[:, k], x_pairs[bass.ds(n, 1)].rearrange("n p h f -> p (n h) f")
                             ).then_inc(loaded[k], 16)

            def store(pair):
                k = pair.k
                sp.wait_ge(x1_done, pair.number(2, 2))
                sp.dma_start(out_pairs[bass.ds(pair.number(), 1)].rearrange("n p h f -> p (n h) f"), x1[:, k]
                             ).then_inc(stored[k], 16)

            def step(pair):
                if (pair + LOAD).exists():
                    load(pair + LOAD)
                if (pair - ADD).exists():
                    store(pair - ADD)

            steps(sp, step, HALF, U, LOAD, first=2)
            for k in range(U):
                sp.wait_ge(stored[k], 16 * (HALF // U))

        @block.gpsimd
        def _(pool):
            pool.memset(minus_half[:], -0.5).then_inc(half_set, 1)
            pool.wait_ge(half_set, 1)

            def residual(pair, h):
                k = pair.k
                pool.wait_ge(gated, pair.number(h + 1, 2))
                if h == 0:
                    after(pool, stored[k], pair.group(U) * 16)
                pool.tensor_tensor(x1[:, k, h, :], branch[:, k % 2, h, :], xin[:, k, h, :],
                                   ALU.add).then_inc(x1_done, 1)

            def scales(pair):
                if (pair + TURN).exists():
                    pool.wait_ge(o_stats, pair.number(2 + 2 * TURN, 2))
                if (pair - RECORD).exists():
                    pool.wait_ge(x1_stats, pair.number(2 - 2 * RECORD, 2))
                norm_scale(pool, st[:, pair.k % 2].rearrange("p a h t s -> p (a h t) s"), small[:, pair.k % 4],
                           1.0, LN_EPS, minus_half, scales_done)

            def step(pair):
                if (pair - ADD).exists():
                    for h in range(2):
                        residual(pair - ADD, h)
                if (pair + TURN).exists() or (pair - RECORD).exists():
                    scales(pair)

            steps(pool, step, HALF, U, TURN, first=2)

        @block.tensor
        def _(pe):
            def tokens(pair, h):
                pe.wait_ge(xn_done, pair.number(h + 1, 2))
                after(pe, xcp_done, pair.number(h, 2))
                for t in range(T):
                    last = pe.transpose(ps_x[:, t * P:(t + 1) * P], xn[:, pair.k % 2, h, t, :], ident[:])
                last.then_inc(xT_done, 1)

            def product(pair, h):
                if h == 0:
                    pe.wait_ge(loaded[pair.k], pair.group(U, 1) * 32)
                after(pe, o_stats, pair.number(h - 1, 2))
                for t in range(T):
                    last = pe.transpose(ps_o[h][:, t * C:(t + 1) * C], prodT[pair.k][:, h, t::T], ident[:])
                last.then_inc(oT_done, 1)

            def gate(pair, h):
                pe.wait_ge(xcp_done, pair.number(h + 1, 2))
                after(pe, gate_done, pair.number(h, 2))
                for t in range(T):
                    last = pe.matmul(ps_g[:, t * C:(t + 1) * C], xnT[pair.k % 2 * 2 + h][:, t * P:(t + 1) * P], wg_c[:],
                                     start=True, stop=True)
                last.then_inc(g_done, 1)

            def outward(pair, h):
                after(pe, gated, pair.number(h - 1, 2))
                for t in range(T):
                    last = pe.matmul(ps_y[h][:, t * C:(t + 1) * C], prodT[pair.k][:, h, t::T], wo_c[:],
                                     start=True, stop=True)
                last.then_inc(y_done, 1)

            def tokens1(pair, h):
                pe.wait_ge(x1n_done, pair.number(h + 1, 2))
                after(pe, x1cp_done, pair.number(h, 2))
                for t in range(T):
                    last = pe.transpose(ps_t[:, t * P:(t + 1) * P], x1n[:, h, t, :], ident[:])
                last.then_inc(x1T_done, 1)

            def expert_logits(pair):
                pe.wait_ge(x1cp_done, pair.number(2, 2))
                after(pe, log_done, pair.number())
                for h in range(2):
                    last = pe.matmul(ps_l[h * E:(h + 1) * E, :], gate_wT[:], x1T[pair.k % 2 * 2 + h][:],
                                     start=True, stop=True)
                last.then_inc(l_done, 1)

            def step(pair):
                turn, weigh, back = pair + TURN, pair + WEIGH, pair - TURN1
                if (pair - LOGITS).exists():
                    expert_logits(pair - LOGITS)
                for h in range(2):
                    for stage, at in ((gate, weigh), (tokens, turn), (product, turn), (tokens1, back),
                                      (outward, weigh)):
                        if at.exists():
                            stage(at, h)

            steps(pe, step, HALF, U, TURN, first=2)

        @block.scalar
        def _(act):
            def normalise(pair, h):
                if h == 0:
                    act.wait_ge(loaded[pair.k], pair.group(U, 1) * 32)
                after(act, xT_done, pair.number(h - 3, 2))
                row = pair.number(h * HALF)
                for t in range(T):
                    last = act.activation(xn[:, pair.k % 2, h, t, :], xin[:, pair.k, h, t * C:(t + 1) * C],
                                          ACT.Identity, bias=x_shift[:, bass.ds(row, 1), t],
                                          scale=x_scale[:, bass.ds(row, 1), t])
                last.then_inc(xn_done, 1)

            def tokens(pair, h):
                act.wait_ge(xT_done, pair.number(h + 1, 2))
                after(act, g_done, pair.number(h - 3, 2))
                act.activation(xnT[pair.k % 2 * 2 + h][:], ps_x[:], ACT.Copy).then_inc(xcp_done, 1)

            def gate(pair, h):
                act.wait_ge(g_done, pair.number(h + 1, 2))
                after(act, gated, pair.number(h - 3, 2))
                act.activation(gates[:, pair.k % 2, h, :], ps_g[:], ACT.Sigmoid).then_inc(gate_done, 1)

            def tokens1(pair, h):
                act.wait_ge(x1T_done, pair.number(h + 1, 2))
                after(act, l_done, pair.number(-1))
                act.activation(x1T[pair.k % 2 * 2 + h][:], ps_t[:], ACT.Copy).then_inc(x1cp_done, 1)

            def expert_logits(pair):
                unit, slot = pair.k % GROUP, pair.k // GROUP
                act.wait_ge(l_done, pair.number(1))
                if unit == 0:
                    after(act, place_done, pair.group(GROUP, -1))
                    after(act, exp_done, pair.group(GROUP, -1))
                act.activation(logits[:, slot, unit * N:(unit + 1) * N].rearrange("e (p t) -> e t p", t=T),
                               ps_l[:].rearrange("e (t p) -> e t p", t=T),
                               ACT.Identity, bias=gate_b2[:]).then_inc(log_done, 1)

            def exponentials(pair):
                g, slot = pair.group(GROUP), pair.k // GROUP
                act.wait_ge(neg_done, pair.group(GROUP, 1))
                act.activation(exps[:], logits[:, slot, :], ACT.Exp, bias=neg_max[:, slot:slot + 1],
                               accum_out=exp_sum[:, bass.ds(g, 1)]).then_inc(exp_done, 1)

            def step(pair):
                turn, weigh, back = pair + TURN, pair + WEIGH, pair - TURN1
                for h in range(2):
                    for stage, at in ((gate, weigh), (tokens, turn), (normalise, pair + NORM), (tokens1, back)):
                        if at.exists():
                            stage(at, h)
                if (pair - LOGITS).exists():
                    expert_logits(pair - LOGITS)
                ended = pair - EXPS
                if ended.exists() and ended.k % GROUP == GROUP - 1:
                    exponentials(ended)

            steps(act, step, HALF, U, NORM, first=2)

        @block.vector
        def _(dve):
            dve.memset(st[:], 0.0).then_inc(st_set, 1)
            dve.wait_ge(st_set, 1)

            def x1_normalise(pair, h):
                s = small[:, (pair.k + RECORD) % 4]
                if h == 0:
                    dve.wait_ge(scales_done, pair.number(1 + RECORD + TURN))
                after(dve, x1T_done, pair.number(h - 1, 2))
                for t in range(T):
                    at = (2 + h) * T + t
                    last = dve.tensor_scalar(x1n[:, h, t, :], x1[:, pair.k, h, t * C:(t + 1) * C],
                                             s[:, 4, at:at + 1], s[:, 3, at:at + 1], ALU.subtract, ALU.mult)
                last.then_inc(x1n_done, 1)

            def x1_records(pair, h):
                dve.wait_ge(x1_done, pair.number(h + 1, 2))
                for t in range(T):
                    last = dve.bn_stats(st[:, (pair.k + RECORD) % 2, 1, h, t, :], x1[:, pair.k, h, t * C:(t + 1) * C])
                last.then_inc(x1_stats, 1)

            def product_records(pair, h):
                dve.wait_ge(oT_done, pair.number(h + 1, 2))
                for t in range(T):
                    last = dve.bn_stats(st[:, pair.k % 2, 0, h, t, :], ps_o[h][:, t * C:(t + 1) * C])
                last.then_inc(o_stats, 1)

            def bias_and_gate(pair, h):
                s = small[:, (pair.k - TURN) % 4]
                dve.wait_ge(y_done, pair.number(h + 1, 2))
                if h == 0:
                    dve.wait_ge(scales_done, pair.number(1))
                y = ps_y[h]
                for t in range(T):
                    at = h * T + t
                    last = dve.scalar_tensor_tensor(y[:, t * C:(t + 1) * C], y[:, t * C:(t + 1) * C],
                                                    s[:, 3, at:at + 1], bo_bc[:], ALU.mult, ALU.add)
                last.then_inc(bias_done, 1)
                dve.wait_ge(gate_done, pair.number(h + 1, 2))
                dve.wait_ge(bias_done, pair.number(h + 1, 2))
                after(dve, x1_done, pair.number(h - 3, 2))
                dve.tensor_tensor(branch[:, pair.k % 2, h, :], y[:], gates[:, pair.k % 2, h, :], ALU.mult).then_inc(gated, 1)

            def largest(pair):
                g, slot = pair.group(GROUP), pair.k // GROUP
                dve.wait_ge(log_done, pair.number(1))
                after(dve, exp_done, pair.group(GROUP, -1))
                dve.memset(neg_max[:, slot:slot + 1], 0.0)
                dve.max(top_v[:, slot, :], logits[:, slot, :]).then_inc(top_found, 1)
                dve.wait_ge(top_found, pair.group(GROUP, 1))
                dve.tensor_scalar(neg_max[:, slot:slot + 1], top_v[:, slot, 0:1], -1.0, None,
                                  ALU.mult).then_inc(neg_done, 1)
                dve.tensor_copy(cand_v[:, bass.ds(g, 1), :].rearrange("p g k -> p (g k)"), top_v[:, slot, :])
                dve.max_index(top_i[:, slot, :], top_v[:, slot, :], logits[:, slot, :]).then_inc(place_done, 1)
                dve.wait_ge(place_done, pair.group(GROUP, 1))
                dve.tensor_copy(cand_i[:, bass.ds(g, 1), :].rearrange("p g k -> p (g k)"), top_i[:, slot, :])

            def step(pair):
                if pair.exists() or (pair + TURN).exists():
                    after(dve, scales_done, pair.number(TURN - 1))
                for stage, at in ((bias_and_gate, pair), (x1_records, pair - RECORD),
                                  (product_records, pair + TURN), (x1_normalise, pair - NORM1)):
                    if at.exists():
                        for h in range(2):
                            stage(at, h)
                ended = pair - SEARCH
                if ended.exists() and ended.k % GROUP == GROUP - 1:
                    largest(ended)

            steps(dve, step, HALF, U, TURN, first=2)


def experts(nc, tensors, out_tokens, ident, cand_v, cand_i, exp_sum, weight1, weight2):
    EG = 8
    EG2 = 4
    S2 = 2
    NC2 = 2 * NG * K
    with ExitStack() as stack:
        sb, pb, sem = tensors(stack)
        w1 = sb("w1", [P, E // EG, EG, H])
        w2 = sb("w2", [P, S2, EG2, HC, O])
        base = sb("base", [P, NG, K])
        mv = sb("mv", [E, 2, NG, K])
        mi = sb("mi", [E, 2, NG, K])
        ms = sb("ms", [E, 2, NG])
        place = sb("place", [E, NC2])
        junk = sb("junk", [E, NC2])
        v8 = sb("v8", [E, K])
        p8 = sb("p8", [E, K], U32)
        p8f = sb("p8f", [E, K])
        idx = sb("idx", [E, K])
        idx_u = sb("idx_u", [E, K], U32)
        negm = sb("negm", [E, 1])
        eg = sb("eg", [E, 2 * NG])
        zsum = sb("zsum", [E, 1])
        zrec = sb("zrec", [E, 1])
        topv = sb("topv", [E, K])
        xg = sb("xg", [E, K, C])
        xgn = sb("xgn", [E, K, C])
        st = sb("st4", [E, K, 6])
        mean_var = sb("mean_var", [E, K, 2])
        half = sb("half4", [E, K])
        var_e = sb("var_e", [E, K])
        rstd = sb("rstd", [E, K])
        nbias = sb("nbias", [E, K])
        pooled = sb("pooled", [E, C])
        pooledT = sb("pooledT", [C, E])
        b1 = sb("b1", [E, H])
        b1T = sb("b1T", [P, HC, E])
        b2 = sb("b2", [E, O])
        h_pre = sb("h_pre", [P, HC, E])
        hT = sb("hT", [P, HC, E])
        oT = sb("oT", [O, E])
        out_e = sb("out_e", [E, O])
        diag = sb("diag", [E, K, E])
        idx_bc = sb("idx_bc", [E, K, E])
        ones = sb("ones4", [E, E])
        lower = sb("lower", [E, E])
        sel = sb("sel", [E, 2, K, E])
        sel_t = sb("sel_t", [E, K, E])
        dup = sb("dup", [E, K])
        idx_s = sb("idx_s", [E, K])
        idx_su = sb("idx_su", [E, K], U32)
        final = sb("final", [E, K, C])
        ps_p = pb("ps4_p", [C, E])
        ps_b = pb("ps4_b", [P, HC * E])
        ps_h = pb("ps4_h", [P, HC * E])
        ps_oT = pb("ps4_oT", [O, E])
        ps_oe = pb("ps4_oe", [E, O])
        ps_i = pb("ps4_i", [E, K * E])
        ps_r = [pb(f"ps4_r{n}", [E, 4 * C]) for n in range(2)]
        w1_in = [sem(f"w1_in{n}") for n in range(E // EG)]
        w2_in = [sem(f"w2_in{n}") for n in range(S2)]
        b_in = sem("b_in")
        v = sem("p4_v")
        pool_s = sem("p4_pool")
        based = sem("p4_based")
        merged = sem("p4_merged")
        max_s = sem("p4_max")
        exp_s = sem("p4_exp")
        idx_s_done = sem("p4_idx")
        gathered = sem("p4_gathered")
        var_s = sem("p4_var")
        rstd_s = sem("p4_rstd")
        pooled_s = sem("p4_pooled")
        pT_s = sem("p4_pT")
        pTc_s = sem("p4_pTc")
        b1T_s = sem("p4_b1T")
        l1_s = sem("p4_l1")
        pre_s = sem("p4_pre")
        gelu_s = sem("p4_gelu")
        l2_s = sem("p4_l2")
        oTc_s = sem("p4_oTc")
        oe_s = sem("p4_oe")
        diag_s = sem("p4_diag")
        ibc_s = sem("p4_ibc")
        sel_s = sem("p4_sel")
        add_s = sem("p4_add")
        scat_i = sem("p4_scat_i")
        final_s = sem("p4_final")
        scattered = sem("p4_scattered")
        block = stack.enter_context(nc.Block())
        GR = E // EG
        GR2 = E // EG2

        @block.sync
        def _(sp):
            sp.dma_start(b1[:], weight1[:, C, :]).then_inc(b_in, 16)
            sp.dma_start(b2[:], weight2[:, H, :]).then_inc(b_in, 16)

            def load1(g, s):
                sp.dma_start(w1[:, s], weight1[bass.ds(g * EG, EG), 0:C, :].rearrange("e d h -> d e h")
                             ).then_inc(w1_in[s], 16)

            def load2(g, s):
                for e in range(EG2):
                    sp.dma_start(w2[:, s, e], weight2[bass.ds(g * EG2 + e, 1), 0:H, :].rearrange(
                        "e (c p) o -> p (e c) o", p=P)).then_inc(w2_in[s], 16)

            sp.wait_ge(based, 1)
            for dst, src in ((mv, cand_v), (mi, cand_i)):
                for h in range(2):
                    sp.dma_start(dst[:, h], src[h * E:(h + 1) * E]).then_inc(merged, 16)
            for h in range(2):
                sp.dma_start(ms[:, h], exp_sum[h * E:(h + 1) * E]).then_inc(merged, 16)
            for g in range(GR):
                load1(g, g)
            for g in range(GR2):
                if g >= S2:
                    sp.wait_ge(l2_s, g - S2 + 1)
                load2(g, g % S2)

        @block.gpsimd
        def _(pool):
            for h in range(2):
                pool.iota(base[h * E:(h + 1) * E], pattern=[[GT, NG], [0, K]], base=h * HALF * N,
                          channel_multiplier=0, allow_small_or_imprecise_dtypes=True)
            pool.iota(place[:], pattern=[[1, NC2]], base=0, channel_multiplier=0,
                      allow_small_or_imprecise_dtypes=True)
            pool.memset(half[:], -0.5)
            pool.memset(ones[:], 1.0).then_inc(pool_s, 1)
            pool.wait_ge(pool_s, 1)
            pool.affine_select(out=lower[:], in_=ones[:], compare_op=ALU.is_gt, fill=0.0, base=0,
                               pattern=[[-1, E]], channel_multiplier=1).then_inc(pool_s, 1)
            pool.wait_ge(idx_s_done, 1)
            for k in range(K):
                pool.indirect_dma_start(out=xg[:, k, :], out_offset=None, in_=out_tokens,
                                        in_offset=bass.IndirectOffsetOnAxis(ap=idx_u[:, k:k + 1], axis=0)
                                        ).then_inc(gathered, 16)
            pool.wait_ge(var_s, 1)
            pool.tensor_tensor(rstd[:], var_e[:], half[:], ALU.pow).then_inc(rstd_s, 1)
            pool.wait_ge(scat_i, 1)
            pool.wait_ge(final_s, 1)
            for k in range(K):
                if k:
                    pool.wait_ge(scattered, 16 * k)
                pool.indirect_dma_start(out=out_tokens,
                                        out_offset=bass.IndirectOffsetOnAxis(ap=idx_su[:, k:k + 1], axis=0),
                                        in_=final[:, k, :], in_offset=None,
                                        bounds_check=TOKENS - 1, oob_is_err=False).then_inc(scattered, 16)
            pool.wait_ge(scattered, 16 * K)

        @block.vector
        def _(dve):
            count = [0]

            def link(ins):
                count[0] += 1
                ins.then_inc(v, 1)
                dve.wait_ge(v, count[0])

            dve.wait_ge(pool_s, 2)
            dve.tensor_tensor(cand_i[:], cand_i[:], base[:], ALU.add).then_inc(based, 1)
            dve.wait_ge(merged, 16 * 6)
            mvf = mv[:].rearrange("e h g k -> e (h g k)")
            mif = mi[:].rearrange("e h g k -> e (h g k)")
            link(dve.max(v8[:], mvf))
            link(dve.max_index(p8[:], v8[:], mvf))
            dve.tensor_scalar(negm[:], v8[:, 0:1], -1.0, None, ALU.mult).then_inc(max_s, 1)
            link(dve.tensor_copy(p8f[:], p8[:]))
            for k in range(K):
                link(dve.scalar_tensor_tensor(junk[:], place[:], p8f[:, k:k + 1], mif, ALU.is_equal, ALU.mult,
                                              accum_out=idx[:, k:k + 1]))
            dve.tensor_copy(idx_u[:], idx[:]).then_inc(idx_s_done, 1)
            dve.wait_ge(exp_s, 2)
            link(dve.tensor_tensor(eg[:], eg[:], ms[:].rearrange("e h g -> e (h g)"), ALU.mult))
            link(dve.reduce_sum(zsum[:], eg[:], axis=AX.X))
            link(dve.reciprocal(zrec[:], zsum[:]))
            link(dve.tensor_scalar(topv[:], topv[:], zrec[:], None, ALU.mult))
            for k in range(K):
                last = dve.tensor_scalar(diag[:, k, :], ident[0:E, 0:E], idx[:, k:k + 1], None, ALU.mult)
            last.then_inc(diag_s, 1)
            dve.wait_ge(ibc_s, 1)
            link(dve.tensor_copy(idx_bc[:], ps_i[:].rearrange("e (k a) -> e k a", k=K)))
            for k in range(K):
                if k == 0:
                    link(dve.tensor_scalar(sel[:, 0], idx_bc[:], idx[:, k:k + 1], topv[:, k:k + 1],
                                           ALU.is_equal, ALU.mult))
                else:
                    link(dve.tensor_scalar(sel_t[:], idx_bc[:], idx[:, k:k + 1], topv[:, k:k + 1],
                                           ALU.is_equal, ALU.mult))
                    link(dve.tensor_tensor(sel[:, k % 2], sel[:, (k - 1) % 2], sel_t[:], ALU.add))
            for k in range(K):
                link(dve.scalar_tensor_tensor(junk[:, 0:E], idx_bc[:, k, :], idx[:, k:k + 1], lower[:],
                                              ALU.is_equal, ALU.mult, accum_out=dup[:, k:k + 1]))
            link(dve.scalar_tensor_tensor(idx_s[:], dup[:], float(TOKENS), idx[:], ALU.mult, ALU.add))
            dve.tensor_copy(idx_su[:], idx_s[:]).then_inc(scat_i, 1)
            dve.wait_ge(gathered, 16 * K)
            for k in range(K):
                last = dve.bn_stats(st[:, k, :], xg[:, k, :])
            link(last)
            for k in range(K):
                last = dve.bn_aggr(mean_var[:, k, :], st[:, k, :])
            link(last)
            dve.tensor_scalar(var_e[:], mean_var[:, :, 1], LN_EPS, None, ALU.add).then_inc(var_s, 1)
            dve.wait_ge(rstd_s, 1)
            link(dve.scalar_tensor_tensor(nbias[:], mean_var[:, :, 0], -1.0, rstd[:], ALU.mult, ALU.mult))
            for k in range(K):
                last = dve.tensor_scalar(xgn[:, k, :], xg[:, k, :], rstd[:, k:k + 1], nbias[:, k:k + 1],
                                         ALU.mult, ALU.add)
            link(last)
            for k in range(K):
                if k == 0:
                    ins = dve.tensor_scalar(pooled[:], xgn[:, k, :], topv[:, k:k + 1], None, ALU.mult)
                else:
                    ins = dve.scalar_tensor_tensor(pooled[:], xgn[:, k, :], topv[:, k:k + 1], pooled[:],
                                                   ALU.mult, ALU.add)
                if k < K - 1:
                    link(ins)
            ins.then_inc(pooled_s, 1)
            dve.wait_ge(pT_s, 1)
            dve.tensor_copy(pooledT[:], ps_p[:]).then_inc(pTc_s, 1)
            dve.wait_ge(b1T_s, 1)
            link(dve.tensor_copy(b1T[:], ps_b[:].rearrange("p (c e) -> p c e", c=HC)))
            dve.wait_ge(l1_s, GR)
            dve.tensor_tensor(h_pre[:], ps_h[:].rearrange("p (c e) -> p c e", c=HC), b1T[:], ALU.add).then_inc(pre_s, 1)
            dve.wait_ge(l2_s, GR2)
            dve.tensor_copy(oT[:], ps_oT[:]).then_inc(oTc_s, 1)
            dve.wait_ge(oe_s, 1)
            dve.tensor_tensor(out_e[:], ps_oe[:], b2[:], ALU.add).then_inc(sel_s, 1)
            dve.wait_ge(add_s, 1)
            for n in range(2):
                last = dve.tensor_tensor(final[:, 4 * n:4 * n + 4, :], ps_r[n][:].rearrange("e (k c) -> e k c", k=4),
                                         xg[:, 4 * n:4 * n + 4, :], ALU.add)
            last.then_inc(final_s, 1)

        @block.scalar
        def _(act):
            act.wait_ge(max_s, 1)
            act.activation(eg[:], mv[:].rearrange("e h g k -> e (h g) k")[:, :, 0], ACT.Exp,
                           bias=negm[:]).then_inc(exp_s, 1)
            act.activation(topv[:], v8[:], ACT.Exp, bias=negm[:]).then_inc(exp_s, 1)
            act.wait_ge(pre_s, 1)
            act.activation(hT[:], h_pre[:], ACT.Gelu).then_inc(gelu_s, 1)

        @block.tensor
        def _(pe):
            pe.wait_ge(diag_s, 1)
            pe.matmul(ps_i[:], ones[:], diag[:].rearrange("e k a -> e (k a)"), start=True, stop=True).then_inc(ibc_s, 1)
            pe.wait_ge(b_in, 32)
            for c in range(HC):
                last = pe.transpose(ps_b[:, c * E:(c + 1) * E], b1[:, c * P:(c + 1) * P], ident[0:E, 0:E])
            last.then_inc(b1T_s, 1)
            pe.wait_ge(pooled_s, 1)
            pe.transpose(ps_p[:], pooled[:], ident[0:E, 0:E]).then_inc(pT_s, 1)
            pe.wait_ge(pTc_s, 1)
            for g in range(GR):
                pe.wait_ge(w1_in[g], 16)
                for x in range(EG):
                    e = g * EG + x
                    for c in range(HC):
                        last = pe.matmul(ps_h[:, c * E + e:c * E + e + 1], w1[:, g, x, c * P:(c + 1) * P],
                                         pooledT[:, e:e + 1], start=True, stop=True)
                last.then_inc(l1_s, 1)
            pe.wait_ge(gelu_s, 1)
            hTf = hT[:].rearrange("p c e -> p (c e)")
            with pe.Fori(0, GR2 // S2) as gg:
                for s in range(S2):
                    pe.wait_ge(w2_in[s], (gg + 1) * 16 * EG2)
                    for x in range(EG2):
                        e = gg * (S2 * EG2) + s * EG2 + x
                        for c in range(HC):
                            last = pe.matmul(ps_oT[:, bass.ds(e, 1)], w2[:, s, x, c, :],
                                             hTf[:, bass.ds(e + c * E, 1)], start=(c == 0), stop=(c == HC - 1))
                    last.then_inc(l2_s, 1)
            pe.wait_ge(oTc_s, 1)
            pe.transpose(ps_oe[:], oT[:], ident[:]).then_inc(oe_s, 1)
            pe.wait_ge(sel_s, 1)
            for k in range(K):
                last = pe.matmul(ps_r[k // 4][:, k % 4 * C:(k % 4 + 1) * C], sel[:, (K - 1) % 2, k, :], out_e[:],
                                 start=True, stop=True)
            last.then_inc(add_s, 1)


_INS = ['x', 'L0_conv_mask', 'L0_conv_ln_g', 'L0_conv_ln_b', 'L0_conv_Wl', 'L0_conv_bl', 'L0_conv_Wr',
        'L0_conv_br', 'L0_conv_Wgl', 'L0_conv_bgl', 'L0_conv_Wgr', 'L0_conv_bgr', 'L0_conv_cg', 'L0_conv_cb',
        'L0_conv_Wo', 'L0_conv_bo', 'L0_conv_Wg', 'L0_conv_bg', 'L0_ffn_gate_w', 'L0_ffn_gate_b',
        'L0_ffn_weight1', 'L0_ffn_weight2']
_OUTS = [((1, N, N, C), 'float32')]


def kernel(**inputs):
    import numpy as _np
    import concourse.bacc as _bacc
    from concourse import mybir as _mybir
    from concourse.bass_utils import run_bass_kernel_spmd as _run

    nc = _bacc.Bacc("TRN2", target_bir_lowering=False, num_devices=1)
    arrays, args = {}, []
    for name in _INS:
        a = _np.ascontiguousarray(inputs[name])
        arrays[f"in_{name}_dram"] = a
        args.append(nc.dram_tensor(f"in_{name}_dram", a.shape, _mybir.dt.from_np(a.dtype), kind="ExternalInput").ap())
    for i, (shape, dtype) in enumerate(_OUTS):
        args.append(nc.dram_tensor(f"out_{i}_dram", shape, _mybir.dt.from_np(_np.dtype(dtype)),
                                   kind="ExternalOutput").ap())
    mk_metaformer(nc, *args)
    r = _run(nc, [arrays], core_ids=[0])
    return r.results[0]["out_0_dram"]
```

```python
import concourse.bass as bass
from concourse import mybir
from contextlib import ExitStack

F32 = mybir.dt.float32
F32R = mybir.dt.float32r
U32 = mybir.dt.uint32
ALU = mybir.AluOpType
ACT = mybir.ActivationFunctionType
AX = mybir.AxisListType

N = 384
C = 128
E, H, O, K = 64, 512, 128, 8
P = 128
T = N // P
TOKENS = N * N
HC = H // P

CW = 8
CG = C // CW
IB = 16
NB = N // IB

CONV_EPS1, CONV_EPS2 = 1e-6, 1e-5
LN_EPS = 1e-5

HALF = N // 2
GROUP = 4
GT = GROUP * N
NG = HALF // GROUP

EG = 8
GR = E // EG


def first_layer(weight1, g):
    return weight1[g * EG:(g + 1) * EG, 0:C, :].rearrange("e d h -> d e h")


def after(eng, sem, count):
    if isinstance(count, int) and count <= 0:
        return
    eng.wait_ge(sem, count)


class Step:

    def __init__(self, q, k, body, count):
        self.q, self.k, self.body, self.count = q, k, body, count

    def __add__(self, more):
        return Step(self.q + (self.k + more) // self.body, (self.k + more) % self.body, self.body, self.count)

    def __sub__(self, less):
        return self + -less

    def number(self, more=0, each=1):
        return self.q * (self.body * each) + (self.k * each + more)

    def group(self, size, more=0):
        return self.q * (self.body // size) + (self.k // size + more)

    def exists(self):
        return not isinstance(self.q, int) or 0 <= self.number() < self.count


def steps(eng, step, count, body, lead, first=1):
    for n in range(-lead, first * body):
        step(Step(n // body, n % body, body, count))
    whole = count // body
    with eng.Fori(first, whole - 1) as q:
        for k in range(body):
            step(Step(q, k, body, count))
    for n in range((whole - 1) * body, (whole + 1) * body):
        step(Step(n // body, n % body, body, count))


def mk_metaformer(nc, x, mask, ln_g, ln_b, Wl, bl, Wr, br, Wgl, bgl, Wgr, bgr, cg, cb, Wo, bo, Wg, bg,
                  gate_w, gate_b, weight1, weight2, out):
    sides_d = nc.dram_tensor("sides_scratch", [2, CG, T, P, NB, IB * CW], F32).ap()
    prod_d = nc.dram_tensor("product_scratch", [C, N, N], F32).ap()

    x_rows = x.rearrange("a i (p t) c -> (a i) p (t c)", t=T)
    out_rows = out.rearrange("a i (p t) c -> (a i) p (t c)", t=T)
    out_tokens = out.rearrange("a i j c -> (a i j) c")

    def tensors(stack):
        def sb(name, shape, dt=F32):
            return stack.enter_context(nc.sbuf_tensor(name, shape, dt))

        def pb(name, shape, dt=F32):
            return stack.enter_context(nc.psum_tensor(name, shape, dt))

        def sem(name):
            return stack.enter_context(nc.semaphore(name))
        return sb, pb, sem

    with ExitStack() as keep:
        sb, _, _ = tensors(keep)
        ident = sb("ident", [P, P])
        wg_c = sb("wg_c", [C, C])
        wo_c = sb("wo_c", [C, C])
        bo_bc = sb("bo_bc", [P, C])
        gate_wT = sb("gate_wT", [C, E])
        gate_b2 = sb("gate_b2", [P, 1])
        x_scale = sb("x_scale", [P, N, T])
        x_shift = sb("x_shift", [P, N, T])
        with ExitStack() as early:
            sb, _, _ = tensors(early)
            w_hi = sb("w_hi", [C, 4 * C], F32R)
            w_lo = sb("w_lo", [C, 4 * C], F32R)
            mask_T = sb("mask_T", [P, T, N])
            prepare(nc, tensors, ident, w_hi, w_lo, wg_c, wo_c, bo_bc, gate_wT, gate_b2, mask_T,
                    mask, ln_g, ln_b, (Wl, Wr, Wgl, Wgr, Wg), (bl, br, bgl, bgr, bg), cg, cb, Wo, bo,
                    gate_w, gate_b)
            project(nc, tensors, x_rows, sides_d, ident, w_hi, w_lo, mask_T, x_scale, x_shift)
        multiply(nc, tensors, sides_d, prod_d)
        sb, _, _ = tensors(keep)
        cand_v = sb("cand_v", [P, NG, K])
        cand_i = sb("cand_i", [P, NG, K])
        exp_sum = sb("exp_sum", [P, NG])
        w1_a = sb("w1_a", [P, GR // 2, EG, H])
        finish_rows(nc, tensors, x_rows, out_rows, prod_d, ident, wg_c, wo_c, bo_bc, gate_wT, gate_b2,
                    x_scale, x_shift, cand_v, cand_i, exp_sum, w1_a, weight1)
        experts(nc, tensors, out_tokens, ident, x_scale, x_shift, cand_v, cand_i, exp_sum, w1_a, weight1,
                weight2)


def prepare(nc, tensors, ident, w_hi, w_lo, wg_c, wo_c, bo_bc, gate_wT, gate_b2, mask_T,
            mask, ln_g, ln_b, weights, biases, cg, cb, Wo, bo, gate_w, gate_b):
    NW = 5 * C
    column = "(c o) -> c o"
    with ExitStack() as stack:
        sb, pb, sem = tensors(stack)
        w_all = sb("w_all", [C, NW])
        wo_raw = sb("wo_raw", [C, C])
        gw_raw = sb("gw_raw", [E, C])
        mask_raw = sb("mask_raw", [P, T, N])
        g_col = sb("g_col", [C, 1])
        b_col = sb("b_col", [C, 1])
        cg_col = sb("cg_col", [C, 1])
        cb_col = sb("cb_col", [C, 1])
        b_row = sb("b_row", [1, NW])
        bo_row = sb("bo_row", [1, C])
        one_row = sb("one_row", [1, P])
        ones = sb("ones", [P, P])
        minus = sb("minus", [P, P])
        b_wide = sb("b_wide", [C, P])
        cb_wide = sb("cb_wide", [C, P])
        wp = sb("wp", [C, NW])
        wop = sb("wop", [C, C])
        wc = sb("wc", [C, NW])
        ps_a = pb("ps_a", [P, 4 * C])
        ps_b = pb("ps_b", [P, C])
        ps_o = pb("ps_o", [P, C])
        ps_bo = pb("ps_bo", [P, C])
        gw_T = sb("gw_T", [C, E])
        ps_g = pb("ps_g", [C, E])
        ps_gm = pb("ps_gm", [C, E])
        ps_m = [pb(f"ps_m{n}", [P, N]) for n in range(2)]
        loaded = sem("prep_loaded")
        ident_done = sem("prep_ident")
        vec = sem("prep_vec")
        folded = sem("prep_folded")
        pe_done = sem("prep_pe")
        mask_pe = sem("prep_mask_pe")
        mask_cp = sem("prep_mask_cp")
        LOADS = 2 * len(weights) + 10
        block = stack.enter_context(nc.Block())

        @block.sync
        def _(sp):
            n = 0
            for at, w in enumerate(weights):
                sp.dma_start(w_all[:, at * C:(at + 1) * C], w).then_inc(loaded, 16)
                sp.dma_start(b_row[0:1, at * C:(at + 1) * C],
                             biases[at].rearrange("(o c) -> o c", o=1)).then_inc(loaded, 16)
                n += 2
            for dst, src in ((wo_raw[:], Wo), (gw_raw[:], gate_w),
                             (mask_raw[:], mask.rearrange("a (r p) j -> p (a r) j", p=P)),
                             (bo_row[:], bo.rearrange("(o c) -> o c", o=1)),
                             (g_col[:], ln_g.rearrange(column, o=1)), (b_col[:], ln_b.rearrange(column, o=1)),
                             (cg_col[:], cg.rearrange(column, o=1)), (cb_col[:], cb.rearrange(column, o=1)),
                             (gate_b2[0:E, :], gate_b.rearrange(column, o=1)),
                             (gate_b2[E:2 * E, :], gate_b.rearrange(column, o=1))):
                sp.dma_start(dst, src).then_inc(loaded, 16)
                n += 1
            assert n == LOADS

        @block.gpsimd
        def _(pool):
            pool.memset(ident[:], 0.0).then_inc(ident_done, 1)
            pool.wait_ge(ident_done, 1)
            pool.affine_select(out=ident[:], in_=ident[:], compare_op=ALU.not_equal, fill=1.0,
                               base=0, pattern=[[-1, P]], channel_multiplier=1).then_inc(ident_done, 1)

        @block.vector
        def _(dve):
            dve.memset(ones[:], 1.0)
            dve.memset(minus[:], -1.0)
            dve.memset(one_row[:], 1.0).then_inc(vec, 1)
            dve.wait_ge(vec, 1)
            dve.wait_ge(loaded, 16 * LOADS)
            dve.tensor_scalar(b_wide[:], ones[:], b_col[:], None, ALU.mult)
            dve.tensor_scalar(cb_wide[:], ones[:], cb_col[:], None, ALU.mult)
            dve.tensor_scalar(wp[:], w_all[:], g_col[:], None, ALU.mult)
            dve.tensor_scalar(wop[:], wo_raw[:], cg_col[:], 2.0, ALU.mult, ALU.mult).then_inc(folded, 1)
            dve.wait_ge(pe_done, 1)
            dve.scalar_tensor_tensor(wc[:, 0:4 * C], ps_a[:], 1.0 / C, wp[:, 0:4 * C], ALU.mult, ALU.add)
            dve.scalar_tensor_tensor(wg_c[:], ps_b[:], 1.0 / C, wp[:, 4 * C:], ALU.mult, ALU.add)
            dve.scalar_tensor_tensor(wo_c[:], ps_o[:], 1.0 / C, wop[:], ALU.mult, ALU.add)
            dve.tensor_copy(bo_bc[:], ps_bo[:])
            dve.tensor_scalar(gw_T[:], ps_g[:], 2.0, None, ALU.mult).then_inc(vec, 1)
            dve.wait_ge(vec, 2)
            dve.tensor_copy(w_hi[:], wc[:, 0:4 * C]).then_inc(vec, 1)
            dve.wait_ge(vec, 3)
            dve.tensor_tensor(w_lo[:], wc[:, 0:4 * C], w_hi[:].bitcast(F32), ALU.subtract)
            dve.wait_ge(pe_done, 2)
            dve.scalar_tensor_tensor(gate_wT[:], ps_gm[:], 1.0 / C, gw_T[:], ALU.mult, ALU.add)
            for t in range(T):
                dve.wait_ge(mask_pe, t + 1)
                dve.tensor_copy(mask_T[:, t, :], ps_m[t % 2][:]).then_inc(mask_cp, 1)

        @block.tensor
        def _(pe):
            pe.wait_ge(ident_done, 2)
            pe.wait_ge(folded, 1)
            pe.matmul(ps_a[:], minus[:], wp[:, 0:4 * C], start=True, stop=False)
            pe.matmul(ps_a[:], b_wide[:], w_all[:, 0:4 * C], start=False, stop=False)
            pe.matmul(ps_a[:], one_row[:], b_row[0:1, 0:4 * C], start=False, stop=True)
            pe.matmul(ps_b[:], minus[:], wp[:, 4 * C:], start=True, stop=False)
            pe.matmul(ps_b[:], b_wide[:], w_all[:, 4 * C:], start=False, stop=False)
            pe.matmul(ps_b[:], one_row[:], b_row[0:1, 4 * C:], start=False, stop=True)
            pe.matmul(ps_o[:], minus[:], wop[:], start=True, stop=True)
            pe.matmul(ps_bo[:], cb_wide[:], wo_raw[:], start=True, stop=False)
            pe.matmul(ps_bo[:], one_row[:], bo_row[:], start=False, stop=True)
            pe.transpose(ps_g[:], gw_raw[:], ident[0:E, 0:E]).then_inc(pe_done, 1)
            pe.wait_ge(vec, 2)
            pe.matmul(ps_gm[:], minus[:], gw_T[:], start=True, stop=True).then_inc(pe_done, 1)
            for t in range(T):
                if t >= 2:
                    pe.wait_ge(mask_cp, t - 1)
                for r in range(T):
                    last = pe.transpose(ps_m[t % 2][:, r * P:(r + 1) * P], mask_raw[:, r, t::T], ident[:])
                last.then_inc(mask_pe, 1)


def norm_scale(pool, st, s, gain, eps, minus_half):
    pool.tensor_tensor(s[:, 0], st[:, :, 1], st[:, :, 4], ALU.add)
    pool.tensor_tensor(s[:, 1], st[:, :, 1], st[:, :, 4], ALU.subtract)
    pool.tensor_tensor(s[:, 2], st[:, :, 2], st[:, :, 5], ALU.add)
    pool.drain()
    pool.tensor_scalar(s[:, 4], s[:, 0], 0.5, 0.0, ALU.mult, ALU.add)
    pool.tensor_scalar(s[:, 1], s[:, 1], (gain ** 0.5) / 2, 0.0, ALU.mult, ALU.add)
    pool.tensor_scalar(s[:, 2], s[:, 2], gain / C, eps, ALU.mult, ALU.add)
    pool.drain()
    pool.tensor_tensor(s[:, 1], s[:, 1], s[:, 1], ALU.mult)
    pool.drain()
    pool.tensor_tensor(s[:, 2], s[:, 2], s[:, 1], ALU.add)
    pool.drain()
    pool.tensor_tensor(s[:, 3], s[:, 2], minus_half[:], ALU.pow)
    pool.drain()


def half_scale(pool, st, s, minus_half, done):
    pool.tensor_tensor(s[:, 1], st[:, :, 1], st[:, :, 4], ALU.subtract)
    pool.tensor_tensor(s[:, 2], st[:, :, 2], st[:, :, 5], ALU.add)
    pool.drain()
    pool.tensor_tensor(s[:, 0], s[:, 1], s[:, 1], ALU.mult)
    pool.tensor_scalar(s[:, 2], s[:, 2], 4.0 / C, 4 * LN_EPS, ALU.mult, ALU.add)
    pool.drain()
    pool.tensor_tensor(s[:, 1], s[:, 2], s[:, 0], ALU.add)
    pool.drain()
    pool.tensor_tensor(s[:, 3], s[:, 1], minus_half[:], ALU.pow).then_inc(done, 1)
    pool.drain()


def project(nc, tensors, x_rows, sides_d, ident, w_hi, w_lo, mask_T, x_scale, x_shift):
    U = IB
    AHEAD_STATS, AHEAD_NORM, AHEAD_T, AHEAD_SPLIT = 8, 3, 2, 1
    with ExitStack() as stack:
        sb, pb, sem = tensors(stack)
        xin = sb("xin", [P, U, T * C])
        st = sb("st", [P, U, T, 6])
        small = sb("small", [P, U // 2, 6, 2 * T])
        minus_half = sb("minus_half", [P, 2 * T])
        xn = sb("xn", [P, U // 2, T, C])
        xT_hi = [sb(f"xT_hi{n}", [C, N], F32R) for n in range(2)]
        xT_lo = [sb(f"xT_lo{n}", [C, N], F32R) for n in range(2)]
        gates = sb("gates", [P, 2 * T, 2 * C])
        stage = sb("stage", [P, 2, T, 2, CG, IB, CW])
        ps_x = [pb(f"ps_x{n}", [C, N]) for n in range(2)]
        ps_w = [pb(f"ps_w{n}", [P, 4 * C]) for n in range(2 * T)]
        x_loaded = [sem(f"x_loaded{n}") for n in range(U // 2)]
        half_set = sem("half_set")
        stats_done = sem("p1_stats")
        scale_done = sem("p1_scale")
        xn_done = sem("p1_xn")
        xn_pool = sem("p1_xn_pool")
        xT_done = sem("p1_xT")
        hi_done = sem("p1_hi")
        lo_done = sem("p1_lo")
        proj_done = sem("p1_proj")
        sig_done = sem("p1_sig")
        gated = sem("p1_gated")
        stored = [sem(f"p1_stored{n}") for n in range(2)]
        block = stack.enter_context(nc.Block())

        @block.sync
        def _(sp):
            def load(pair, k):
                after(sp, xT_done, pair * 2 + (2 - U))
                sp.dma_start(xin[:, 2 * k:2 * k + 2, :],
                             x_rows[bass.ds(pair * 2, 2)].rearrange("r p n -> p r n")).then_inc(x_loaded[k], 16)

            PAIRS = IB // 2
            AHEAD = 6

            def store(b, buf, piece):
                t, side = divmod(piece, 2)
                if piece == 0:
                    sp.wait_ge(gated, (b + 1) * IB * T)
                sp.dma_start(sides_d[side, :, t, :, bass.ds(b, 1), :].rearrange("g p b n -> p g (b n)"),
                             stage[:, buf, t, side].rearrange("p g i c -> p g (i c)")).then_inc(stored[buf], 16)

            def block_of_rows(b, buf):
                for j in range(PAIRS):
                    if not isinstance(b, int) or b * PAIRS + j + AHEAD < N // 2:
                        load(b * PAIRS + j + AHEAD, (j + AHEAD) % PAIRS)
                    if j < 2 * T and (not isinstance(b, int) or b > 0):
                        store(b - 1, 1 - buf, j)

            for pair in range(AHEAD):
                load(pair, pair)
            for b in range(2):
                block_of_rows(b, b)
            with sp.Fori(1, NB // 2 - 1) as bb:
                for buf in range(2):
                    block_of_rows(bb * 2 + buf, buf)
            for b in range(NB - 2, NB):
                block_of_rows(b, b % 2)
            for piece in range(2 * T):
                store(NB - 1, (NB - 1) % 2, piece)
            for buf in range(2):
                sp.wait_ge(stored[buf], 16 * 2 * T * (NB // 2))

        @block.vector
        def _(dve):
            dve.memset(minus_half[:], -0.5).then_inc(half_set, 1)

            def stats(row):
                k = row.k
                dve.wait_ge(x_loaded[k // 2], row.group(U, 1) * 16)
                after(dve, scale_done, row.group(2, 1 - U // 2))
                for t in range(T):
                    last = dve.bn_stats(st[:, k, t, :], xin[:, k, t * C:(t + 1) * C])
                last.then_inc(stats_done, 1)

            def split(row):
                dve.wait_ge(hi_done, row.number(1))
                after(dve, proj_done, row.number(-T, T))
                par = row.k % 2
                dve.tensor_tensor(xT_lo[par][:], ps_x[par][:], xT_hi[par][:].bitcast(F32),
                                  ALU.subtract).then_inc(lo_done, 1)

            def gate(row):
                k, q = row.k, row.q
                buf, ii = (q // (IB // U)) % 2, (q % (IB // U)) * U + k
                if k == 0:
                    after(dve, stored[0], q // (2 * IB // U) * (16 * 2 * T))
                    after(dve, stored[1], (q - IB // U) // (2 * IB // U) * (16 * 2 * T))
                for t in range(T):
                    tile = k % 2 * T + t
                    dve.wait_ge(sig_done, row.number(t + 1, T))
                    dve.scalar_tensor_tensor(
                        stage[:, bass.ds(buf, 1), t, :, :, bass.ds(ii, 1), :].rearrange(
                            "p b s g i c -> p (b s g) (i c)"),
                        ps_w[tile][:, 0:2 * C].rearrange("p (g c) -> p g c", c=CW),
                        mask_T[:, t, bass.ds(row.number(), 1)],
                        gates[:, tile, :].rearrange("p (g c) -> p g c", c=CW),
                        ALU.mult, ALU.mult).then_inc(gated, 1)

            def step(row):
                if (row + AHEAD_SPLIT).exists():
                    split(row + AHEAD_SPLIT)
                if row.exists():
                    gate(row)
                if (row + AHEAD_STATS).exists():
                    stats(row + AHEAD_STATS)

            steps(dve, step, N, U, AHEAD_STATS, first=2)

        @block.gpsimd
        def _(pool):
            pool.wait_ge(half_set, 1)

            def scales(row):
                k = row.k
                s = small[:, k // 2]
                pool.wait_ge(stats_done, row.number(2))
                after(pool, xn_done, row.number(2 - U))
                after(pool, xT_done, row.number(2 - U // 2))
                norm_scale(pool, st[:, k:k + 2].rearrange("p r t s -> p (r t) s"), s,
                           1.0 + CONV_EPS2, CONV_EPS1 * CONV_EPS2, minus_half)
                pool.tensor_tensor(s[:, 4], s[:, 4], s[:, 3], ALU.mult)
                pool.drain()
                pool.tensor_scalar(s[:, 5], s[:, 4], -1.0, 1.0, ALU.mult, ALU.add).then_inc(scale_done, 1)
                pool.drain()
                at = 2 * T - 1
                pool.tensor_scalar(xn[:, (k + 1) % (U // 2), T - 1, :], xin[:, k + 1, (T - 1) * C:T * C],
                                   s[:, 3, at:at + 1], s[:, 5, at:at + 1], ALU.mult, ALU.add).then_inc(xn_pool, 1)
                pool.tensor_copy(x_scale[:, bass.ds(row.number(), 2), :], s[:, 3].rearrange("p (r t) -> p r t", t=T))
                pool.tensor_copy(x_shift[:, bass.ds(row.number(), 2), :], s[:, 5].rearrange("p (r t) -> p r t", t=T))

            def step(row):
                if (row + AHEAD_STATS).exists() and row.k % 2 == 0:
                    scales(row + AHEAD_STATS)

            steps(pool, step, N, U, AHEAD_STATS)

        @block.tensor
        def _(pe):
            def transposes(row):
                k = row.k
                pe.wait_ge(xn_done, row.number(1))
                if k % 2:
                    pe.wait_ge(xn_pool, row.group(2, 1))
                after(pe, lo_done, row.number(-1))
                for t in range(T):
                    last = pe.transpose(ps_x[k % 2][:, t * P:(t + 1) * P], xn[:, k % (U // 2), t, :], ident[:])
                last.then_inc(xT_done, 1)

            def projections(row):
                k = row.k
                hi, lo = xT_hi[k % 2], xT_lo[k % 2]
                pe.wait_ge(lo_done, row.number(1))
                for t in range(T):
                    dst = ps_w[k % 2 * T + t]
                    at = slice(t * P, (t + 1) * P)
                    after(pe, gated, row.number(t + 1 - 2 * T, T))
                    pe.matmul(dst[:], hi[:, at], w_hi[:], start=True, stop=False)
                    pe.matmul(dst[:], hi[:, at], w_lo[:], start=False, stop=False)
                    pe.matmul(dst[:], lo[:, at], w_hi[:], start=False, stop=True).then_inc(proj_done, 1)

            def step(row):
                if (row + AHEAD_T).exists():
                    transposes(row + AHEAD_T)
                if row.exists():
                    projections(row)

            steps(pe, step, N, U, AHEAD_T)

        @block.scalar
        def _(act):
            def normalise(row):
                k = row.k
                act.wait_ge(scale_done, row.group(2, 1))
                after(act, xT_done, row.number(1 - U // 2))
                s = small[:, k // 2]
                for t in range(T - k % 2):
                    at = k % 2 * T + t
                    last = act.activation(xn[:, k % (U // 2), t, :], xin[:, k, t * C:(t + 1) * C], ACT.Identity,
                                          bias=s[:, 5, at:at + 1], scale=s[:, 3, at:at + 1])
                last.then_inc(xn_done, 1)

            def upper(row):
                k = row.k
                act.wait_ge(xT_done, row.number(1))
                after(act, proj_done, row.number(-T, T))
                act.activation(xT_hi[k % 2][:], ps_x[k % 2][:], ACT.Copy).then_inc(hi_done, 1)

            def sigmoids(row):
                for t in range(T):
                    tile = row.k % 2 * T + t
                    act.wait_ge(proj_done, row.number(t + 1, T))
                    act.activation(gates[:, tile, :], ps_w[tile][:, 2 * C:4 * C],
                                   ACT.Sigmoid).then_inc(sig_done, 1)

            def step(row):
                if (row + AHEAD_SPLIT).exists():
                    upper(row + AHEAD_SPLIT)
                if (row + AHEAD_NORM).exists():
                    normalise(row + AHEAD_NORM)
                if row.exists():
                    sigmoids(row)

            steps(act, step, N, U, AHEAD_NORM)


def multiply(nc, tensors, sides_d, prod_d):
    RT = N // P
    U = 2
    with ExitStack() as stack:
        sb, pb, sem = tensors(stack)
        raw = sb("raw", [P, 2, 2, T, N, CW])
        hi = [sb(f"hi{n}", [P, 2, T, N], F32R) for n in range(U)]
        lo = [sb(f"lo{n}", [P, 2, T, N], F32R) for n in range(U)]
        prod = sb("prod", [P, U, RT, N])
        ps = [pb(f"ps_p{n}", [P, N]) for n in range(U * RT)]
        loaded = [sem(f"p2_loaded{n}") for n in range(2)]
        hi_done = sem("p2_hi")
        lo_done = sem("p2_lo")
        summed = sem("p2_summed")
        copied_a = sem("p2_copied_a")
        copied_v = sem("p2_copied_v")
        stored = [sem(f"p2_stored{n}") for n in range(U)]
        block = stack.enter_context(nc.Block())

        @block.sync
        def _(sp):
            def load(g, buf):
                for piece in range(2 * T):
                    side, t = divmod(piece, T)
                    after(sp, lo_done, (g - 1) * (2 * CW) + 2 * piece + 2 * min(piece, 1))
                    sp.dma_start(raw[:, buf, side, t].rearrange("p i c -> p (i c)"),
                                 sides_d[side, bass.ds(g, 1), t].rearrange("g p b n -> p (g b n)")
                                 ).then_inc(loaded[buf], 16)

            load(0, 0)
            load(1, 1)
            with sp.Fori(1, CG // 2) as gg:
                for buf in range(2):
                    load(gg * 2 + buf, buf)

        def part(ch, side):
            c = ch.number()
            v = raw[:, bass.ds((c // CW) % 2, 1), side, :, :, bass.ds(c % CW, 1)]
            return v.rearrange("p b t i c -> p (b t) (i c)")

        @block.scalar
        def _(act):
            def upper(ch):
                if ch.k == 0:
                    g = ch.number() // CW
                    act.wait_ge(loaded[0], (g + 2) // 2 * (16 * 2 * T))
                    after(act, loaded[1], (g + 1) // 2 * (16 * 2 * T))
                after(act, summed, ch.number(-RT, RT))
                for side in range(2):
                    act.activation(hi[ch.k][:, side], part(ch, side), ACT.Copy).then_inc(hi_done, 1)

            def copy(ch):
                act.wait_ge(summed, ch.number(1, RT))
                after(act, stored[ch.k], ch.group(U) * 16)
                act.activation(prod[:, ch.k, 0, :], ps[ch.k * RT][:], ACT.Copy).then_inc(copied_a, 1)

            def store(ch):
                act.wait_ge(copied_a, ch.number(1))
                act.wait_ge(copied_v, ch.number(1))
                act.dma_start(prod_d[bass.ds(ch.number(), 1)].rearrange("c (r p) j -> p (c r) j", p=P),
                              prod[:, ch.k]).then_inc(stored[ch.k], 16)

            def step(ch):
                if (ch + 1).exists():
                    upper(ch + 1)
                if (ch - 1).exists():
                    store(ch - 1)
                if ch.exists():
                    copy(ch)

            steps(act, step, C, U, 1)
            for k in range(U):
                act.wait_ge(stored[k], 16 * (C // U))

        @block.vector
        def _(dve):
            def lower(ch):
                for side in range(2):
                    dve.wait_ge(hi_done, ch.number(side + 1, 2))
                    if side == 0:
                        after(dve, summed, ch.number(-RT, RT))
                    dve.tensor_tensor(lo[ch.k][:, side], part(ch, side), hi[ch.k][:, side].bitcast(F32),
                                      ALU.subtract).then_inc(lo_done, 1)

            def copy(ch):
                for r in range(1, RT):
                    dve.wait_ge(summed, ch.number(r + 1, RT))
                    if r == 1:
                        after(dve, stored[ch.k], ch.group(U) * 16)
                    last = dve.tensor_copy(prod[:, ch.k, r, :], ps[ch.k * RT + r][:])
                last.then_inc(copied_v, 1)

            def step(ch):
                if (ch + 1).exists():
                    lower(ch + 1)
                if ch.exists():
                    copy(ch)

            steps(dve, step, C, U, 1)

        @block.tensor
        def _(pe):
            def step(ch):
                if not ch.exists():
                    return
                k = ch.k
                pe.wait_ge(lo_done, ch.number(2, 2))
                after(pe, copied_a, ch.number(1 - U))
                after(pe, copied_v, ch.number(1 - U))
                for r in range(RT):
                    at = slice(r * P, (r + 1) * P)
                    for t in range(T):
                        pe.matmul(ps[k * RT + r][:], hi[k][:, 0, t, at], hi[k][:, 1, t, :],
                                  start=(t == 0), stop=False)
                        pe.matmul(ps[k * RT + r][:], hi[k][:, 0, t, at], lo[k][:, 1, t, :],
                                  start=False, stop=False)
                        last = pe.matmul(ps[k * RT + r][:], lo[k][:, 0, t, at], hi[k][:, 1, t, :],
                                         start=False, stop=(t == T - 1))
                    last.then_inc(summed, 1)

            steps(pe, step, C, U, 0)


def finish_rows(nc, tensors, x_rows, out_rows, prod_d, ident, wg_c, wo_c, bo_bc, gate_wT, gate_b2,
                x_scale, x_shift, cand_v, cand_i, exp_sum, w1_a, weight1):
    U = 2 * GROUP
    LOAD, NORM, TURN, WEIGH = 6, 3, 2, 1
    ADD, RECORD, NORM1, TURN1, LOGITS, SEARCH, PLACES, EXPS = 1, 2, 4, 5, 6, 7, 8, 8
    x_pairs = x_rows.rearrange("(h n) p f -> n p h f", h=2)
    out_pairs = out_rows.rearrange("(h n) p f -> n p h f", h=2)
    prod_pairs = prod_d.rearrange("c (h n) j -> n c h j", h=2)
    with ExitStack() as stack:
        sb, pb, sem = tensors(stack)
        prodT = [sb(f"prodT{n}", [C, 2, N]) for n in range(U)]
        xin = sb("x3", [P, U, 2, T * C])
        xn = sb("xn3", [P, 2, 2, T, C])
        xnT = [sb(f"xnT{n}", [C, N]) for n in range(4)]
        gates = sb("gates3", [P, 2, 2, T * C])
        branch = sb("branch", [P, 2, 2, T * C])
        x1 = sb("x1", [P, U, 2, T * C])
        st = sb("st3", [P, 2, 2, 2, T, 6])
        small = sb("small3", [P, 4, 5, 4 * T])
        minus_half = sb("minus_half3", [P, 4 * T])
        x1n = sb("x1n", [P, 2, 2, T, C])
        x1T = [sb(f"x1T{n}", [C, N]) for n in range(4)]
        logits = sb("logits", [P, 2, GT])
        top_v = sb("top_v", [P, 2, K])
        top_i = sb("top_i", [P, 2, K], U32)
        neg_max = sb("neg_max", [P, 2])
        exps = sb("exps", [P, GT])
        ps_x = pb("ps3_x", [C, N])
        ps_g = pb("ps3_g", [P, N])
        ps_o = [pb(f"ps3_o{n}", [P, N]) for n in range(2)]
        ps_y = [pb(f"ps3_y{n}", [P, N]) for n in range(2)]
        ps_t = pb("ps3_t", [C, N])
        ps_l = pb("ps3_l", [P, N])
        loaded = [sem(f"p3_loaded{n}") for n in range(U)]
        stored = [sem(f"p3_stored{n}") for n in range(U)]
        half_set = sem("p3_half")
        st_set = sem("p3_st")
        w1_in = sem("p3_w1")
        xn_done = sem("p3_xn")
        scales_done = sem("p3_scales")
        x1_done = sem("p3_x1")
        x1n_done = sem("p3_x1n")
        x1n_pool = sem("p3_x1n_pool")
        xT_done = sem("p3_xT")
        oT_done = sem("p3_oT")
        g_done = sem("p3_g")
        y_done = sem("p3_y")
        x1T_done = sem("p3_x1T")
        l_done = sem("p3_l")
        xcp_done = sem("p3_xcp")
        gate_done = sem("p3_gate")
        x1cp_done = sem("p3_x1cp")
        log_done = sem("p3_log")
        o_stats = sem("p3_ostats")
        x1_stats = sem("p3_x1stats")
        bias_done = sem("p3_bias")
        gated = sem("p3_gated")
        exp_done = sem("p3_exp")
        top_found = sem("p3_top")
        neg_done = sem("p3_neg")
        place_done = sem("p3_place")
        block = stack.enter_context(nc.Block())

        def over_std(eng, pair, h):
            s = small[:, (pair.k + RECORD) % 4]
            return eng.tensor_tensor(x1n[:, pair.k % 2, h], x1[:, pair.k, h].rearrange("p (t c) -> p t c", c=C),
                                     s[:, 3, (2 + h) * T:(3 + h) * T].rearrange("p (n o) -> p n o", o=1)
                                     .broadcast_to([P, T, C]), ALU.mult)

        @block.sync
        def _(sp):
            def load(pair):
                k = pair.k
                after(sp, y_done, pair.number(2 - 2 * U, 2))
                after(sp, x1_done, pair.number(2 - 2 * U, 2))
                n = pair.number()
                sp.dma_start(prodT[k][:], prod_pairs[bass.ds(n, 1)].rearrange("n c h j -> c (n h) j")
                             ).then_inc(loaded[k], 16)
                sp.dma_start(xin[:, k], x_pairs[bass.ds(n, 1)].rearrange("n p h f -> p (n h) f")
                             ).then_inc(loaded[k], 16)

            def store(pair):
                k = pair.k
                sp.wait_ge(x1_done, pair.number(2, 2))
                sp.dma_start(out_pairs[bass.ds(pair.number(), 1)].rearrange("n p h f -> p (n h) f"), x1[:, k]
                             ).then_inc(stored[k], 16)

            def step(pair):
                if (pair + LOAD).exists():
                    load(pair + LOAD)
                if (pair - ADD).exists():
                    store(pair - ADD)
                if isinstance(pair.q, int) and 0 <= pair.number() < GR // 2:
                    sp.dma_start(w1_a[:, pair.number()], first_layer(weight1, pair.number())).then_inc(w1_in, 16)

            steps(sp, step, HALF, U, LOAD, first=2)
            sp.wait_ge(w1_in, 16 * (GR // 2))
            for k in range(U):
                sp.wait_ge(stored[k], 16 * (HALF // U))

        @block.gpsimd
        def _(pool):
            pool.memset(minus_half[:], -0.5).then_inc(half_set, 1)
            pool.wait_ge(half_set, 1)

            def residual(pair, h):
                k = pair.k
                pool.wait_ge(gated, pair.number(h + 1, 2))
                if h == 0:
                    after(pool, stored[k], pair.group(U) * 16)
                pool.tensor_tensor(x1[:, k, h, :], branch[:, k % 2, h, :], xin[:, k, h, :],
                                   ALU.add).then_inc(x1_done, 1)

            def scales(pair):
                if (pair + TURN).exists():
                    pool.wait_ge(o_stats, pair.number(2 + 2 * TURN, 2))
                if (pair - RECORD).exists():
                    pool.wait_ge(x1_stats, pair.number(2 - 2 * RECORD, 2))
                half_scale(pool, st[:, pair.k % 2].rearrange("p a h t s -> p (a h t) s"), small[:, pair.k % 4],
                           minus_half, scales_done)

            def step(pair):
                if (pair - ADD).exists():
                    for h in range(2):
                        residual(pair - ADD, h)
                if (pair - NORM1).exists():
                    after(pool, x1T_done, (pair - NORM1).number(-2, 2))
                    over_std(pool, pair - NORM1, 1).then_inc(x1n_pool, 1)
                if (pair + TURN).exists() or (pair - RECORD).exists():
                    scales(pair)

            steps(pool, step, HALF, U, TURN, first=2)

        @block.tensor
        def _(pe):
            def tokens(pair, h):
                pe.wait_ge(xn_done, pair.number(h + 1, 2))
                after(pe, xcp_done, pair.number(h, 2))
                for t in range(T):
                    last = pe.transpose(ps_x[:, t * P:(t + 1) * P], xn[:, pair.k % 2, h, t, :], ident[:])
                last.then_inc(xT_done, 1)

            def product(pair, h):
                if h == 0:
                    pe.wait_ge(loaded[pair.k], pair.group(U, 1) * 32)
                after(pe, o_stats, pair.number(h - 1, 2))
                for t in range(T):
                    last = pe.transpose(ps_o[h][:, t * C:(t + 1) * C], prodT[pair.k][:, h, t::T], ident[:])
                last.then_inc(oT_done, 1)

            def gate(pair, h):
                pe.wait_ge(xcp_done, pair.number(h + 1, 2))
                after(pe, gate_done, pair.number(h, 2))
                for t in range(T):
                    last = pe.matmul(ps_g[:, t * C:(t + 1) * C], xnT[pair.k % 2 * 2 + h][:, t * P:(t + 1) * P], wg_c[:],
                                     start=True, stop=True)
                last.then_inc(g_done, 1)

            def outward(pair, h):
                after(pe, gated, pair.number(h - 1, 2))
                for t in range(T):
                    last = pe.matmul(ps_y[h][:, t * C:(t + 1) * C], prodT[pair.k][:, h, t::T], wo_c[:],
                                     start=True, stop=True)
                last.then_inc(y_done, 1)

            def tokens1(pair, h):
                pe.wait_ge((x1n_done, x1n_pool)[h], pair.number(1))
                after(pe, x1cp_done, pair.number(h, 2))
                for t in range(T):
                    last = pe.transpose(ps_t[:, t * P:(t + 1) * P], x1n[:, pair.k % 2, h, t, :], ident[:])
                last.then_inc(x1T_done, 1)

            def expert_logits(pair):
                pe.wait_ge(x1cp_done, pair.number(2, 2))
                after(pe, log_done, pair.number())
                for h in range(2):
                    last = pe.matmul(ps_l[h * E:(h + 1) * E, :], gate_wT[:], x1T[pair.k % 2 * 2 + h][:],
                                     start=True, stop=True)
                last.then_inc(l_done, 1)

            def step(pair):
                turn, weigh, back = pair + TURN, pair + WEIGH, pair - TURN1
                for h in range(2):
                    for stage, at in ((gate, weigh), (tokens, turn), (product, turn), (tokens1, back)):
                        if at.exists():
                            stage(at, h)
                    if h == 0 and (pair - LOGITS).exists():
                        expert_logits(pair - LOGITS)
                if weigh.exists():
                    for h in range(2):
                        outward(weigh, h)

            steps(pe, step, HALF, U, TURN, first=2)

        @block.scalar
        def _(act):
            def normalise(pair, h):
                if h == 0:
                    act.wait_ge(loaded[pair.k], pair.group(U, 1) * 32)
                after(act, xT_done, pair.number(h - 3, 2))
                row = pair.number(h * HALF)
                for t in range(T):
                    last = act.activation(xn[:, pair.k % 2, h, t, :], xin[:, pair.k, h, t * C:(t + 1) * C],
                                          ACT.Identity, bias=x_shift[:, bass.ds(row, 1), t],
                                          scale=x_scale[:, bass.ds(row, 1), t])
                last.then_inc(xn_done, 1)

            def tokens(pair, h):
                act.wait_ge(xT_done, pair.number(h + 1, 2))
                after(act, g_done, pair.number(h - 3, 2))
                act.activation(xnT[pair.k % 2 * 2 + h][:], ps_x[:], ACT.Copy).then_inc(xcp_done, 1)

            def gate(pair, h):
                act.wait_ge(g_done, pair.number(h + 1, 2))
                after(act, gated, pair.number(h - 3, 2))
                act.activation(gates[:, pair.k % 2, h, :], ps_g[:], ACT.Sigmoid).then_inc(gate_done, 1)

            def tokens1(pair, h):
                act.wait_ge(x1T_done, pair.number(h + 1, 2))
                after(act, l_done, pair.number(-1))
                act.activation(x1T[pair.k % 2 * 2 + h][:], ps_t[:], ACT.Copy).then_inc(x1cp_done, 1)

            def expert_logits(pair):
                unit, slot = pair.k % GROUP, pair.k // GROUP
                act.wait_ge(l_done, pair.number(1))
                if unit == 0:
                    after(act, place_done, pair.group(GROUP, -1))
                    after(act, exp_done, pair.group(GROUP, -1))
                act.activation(logits[:, slot, unit * N:(unit + 1) * N].rearrange("e (p t) -> e t p", t=T),
                               ps_l[:].rearrange("e (t p) -> e t p", t=T),
                               ACT.Identity, bias=gate_b2[:]).then_inc(log_done, 1)

            def exponentials(pair):
                g, slot = pair.group(GROUP), pair.k // GROUP
                act.wait_ge(neg_done, pair.group(GROUP, 1))
                act.activation(exps[:], logits[:, slot, :], ACT.Exp, bias=neg_max[:, slot:slot + 1],
                               accum_out=exp_sum[:, bass.ds(g, 1)]).then_inc(exp_done, 1)

            def step(pair):
                turn, weigh, back = pair + TURN, pair + WEIGH, pair - TURN1
                for h in range(2):
                    for stage, at in ((gate, weigh), (tokens, turn), (normalise, pair + NORM), (tokens1, back)):
                        if at.exists():
                            stage(at, h)
                if (pair - LOGITS).exists():
                    expert_logits(pair - LOGITS)
                ended = pair - EXPS
                if ended.exists() and ended.k % GROUP == GROUP - 1:
                    exponentials(ended)

            steps(act, step, HALF, U, NORM, first=2)

        @block.vector
        def _(dve):
            dve.memset(st[:], 0.0).then_inc(st_set, 1)
            dve.wait_ge(st_set, 1)

            def x1_normalise(pair):
                dve.wait_ge(scales_done, pair.number(1 + RECORD + TURN))
                after(dve, x1T_done, pair.number(-3, 2))
                over_std(dve, pair, 0).then_inc(x1n_done, 1)

            def x1_records(pair, h):
                dve.wait_ge(x1_done, pair.number(h + 1, 2))
                for t in range(T):
                    last = dve.bn_stats(st[:, (pair.k + RECORD) % 2, 1, h, t, :], x1[:, pair.k, h, t * C:(t + 1) * C])
                last.then_inc(x1_stats, 1)

            def product_records(pair, h):
                dve.wait_ge(oT_done, pair.number(h + 1, 2))
                for t in range(T):
                    last = dve.bn_stats(st[:, pair.k % 2, 0, h, t, :], ps_o[h][:, t * C:(t + 1) * C])
                last.then_inc(o_stats, 1)

            def bias(pair, h):
                s = small[:, (pair.k - TURN) % 4]
                dve.wait_ge(y_done, pair.number(h + 1, 2))
                if h == 0:
                    dve.wait_ge(scales_done, pair.number(1))
                y = ps_y[h]
                for t in range(T):
                    at = h * T + t
                    last = dve.scalar_tensor_tensor(y[:, t * C:(t + 1) * C], y[:, t * C:(t + 1) * C],
                                                    s[:, 3, at:at + 1], bo_bc[:], ALU.mult, ALU.add)
                last.then_inc(bias_done, 1)

            def apply_gate(pair, h):
                dve.wait_ge(gate_done, pair.number(h + 1, 2))
                dve.wait_ge(bias_done, pair.number(h + 1, 2))
                after(dve, x1_done, pair.number(h - 3, 2))
                dve.tensor_tensor(branch[:, pair.k % 2, h, :], ps_y[h][:], gates[:, pair.k % 2, h, :],
                                  ALU.mult).then_inc(gated, 1)

            def largest(pair):
                g, slot = pair.group(GROUP), pair.k // GROUP
                dve.wait_ge(log_done, pair.number(1))
                after(dve, exp_done, pair.group(GROUP, -1))
                dve.memset(neg_max[:, slot:slot + 1], 0.0)
                dve.max(top_v[:, slot, :], logits[:, slot, :]).then_inc(top_found, 1)
                dve.wait_ge(top_found, pair.group(GROUP, 1))
                dve.tensor_scalar(neg_max[:, slot:slot + 1], top_v[:, slot, 0:1], -1.0, None,
                                  ALU.mult).then_inc(neg_done, 1)
                dve.tensor_copy(cand_v[:, bass.ds(g, 1), :].rearrange("p g k -> p (g k)"), top_v[:, slot, :])

            def places(pair):
                g, slot = pair.group(GROUP), pair.k // GROUP
                dve.max_index(top_i[:, slot, :], top_v[:, slot, :], logits[:, slot, :]).then_inc(place_done, 1)
                dve.wait_ge(place_done, pair.group(GROUP, 1))
                dve.tensor_copy(cand_i[:, bass.ds(g, 1), :].rearrange("p g k -> p (g k)"), top_i[:, slot, :])

            def step(pair):
                if pair.exists() or (pair + TURN).exists():
                    after(dve, scales_done, pair.number(TURN - 1))
                for stage, at in ((bias, pair), (apply_gate, pair), (x1_records, pair - RECORD)):
                    if at.exists():
                        for h in range(2):
                            stage(at, h)
                if (pair - NORM1).exists():
                    x1_normalise(pair - NORM1)
                if (pair + TURN).exists():
                    for h in range(2):
                        product_records(pair + TURN, h)
                ended = pair - SEARCH
                if ended.exists() and ended.k % GROUP == GROUP - 1:
                    largest(ended)
                ended = pair - PLACES
                if ended.exists() and ended.k % GROUP == GROUP - 1:
                    places(ended)

            steps(dve, step, HALF, U, TURN, first=2)


def experts(nc, tensors, out_tokens, ident, x_scale, x_shift, cand_v, cand_i, exp_sum, w1_a, weight1,
            weight2):
    EW = 32
    NC2 = 2 * NG * K
    with ExitStack() as stack:
        sb, pb, sem = tensors(stack)
        w1_b = sb("w1_b", [P, GR // 2, EG, H])
        spread = sb("spread", [P, HC, E * EW])
        base = sb("base", [P, NG, K])
        mv = sb("mv", [E, 2, NG, K])
        mi = sb("mi", [E, 2, NG, K])
        ms = sb("ms", [E, 2, NG])
        place = x_scale[0:E].rearrange("p n t -> p (n t)")[:, 0:NC2]
        junk = x_shift[0:E].rearrange("p n t -> p (n t)")[:, 0:NC2]
        v8 = sb("v8", [E, K])
        p8 = sb("p8", [E, K], U32)
        p8f = sb("p8f", [E, K])
        idx = sb("idx", [E, K])
        idx_u = sb("idx_u", [E, K], U32)
        negm = sb("negm", [E, 1])
        eg = sb("eg", [E, 2 * NG])
        zsum = sb("zsum", [E, 1])
        zrec = sb("zrec", [E, 1])
        topv = sb("topv", [E, K])
        xg = sb("xg", [E, K, C])
        xgn = sb("xgn", [E, K, C])
        st = sb("st4", [E, K, 6])
        mean_var = sb("mean_var", [E, K, 2])
        half = sb("half4", [E, K])
        var_e = sb("var_e", [E, K])
        rstd = sb("rstd", [E, K])
        nbias = sb("nbias", [E, K])
        pooled = sb("pooled", [E, C])
        b1 = sb("b1", [E, H])
        b2 = sb("b2", [E, O])
        h_pre = sb("h_pre", [E, H])
        out_e = sb("out_e", [E, O])
        diag = sb("diag", [E, K, E])
        idx_bc = sb("idx_bc", [E, K, E])
        ones = sb("ones4", [E, E])
        lower = sb("lower", [E, E])
        sel = sb("sel", [E, 2, K, E])
        sel_t = diag
        dup = sb("dup", [E, K])
        idx_s = sb("idx_s", [E, K])
        idx_su = sb("idx_su", [E, K], U32)
        ps_p = pb("ps4_p", [C, E])
        ps_b = pb("ps4_b", [P, HC * E])
        ps_h = pb("ps4_h", [E, H])
        ps_oe = pb("ps4_oe", [E, O])
        ps_i = pb("ps4_i", [E, K * E])
        ps_r = [pb(f"ps4_r{n}", [E, 4 * C]) for n in range(2)]
        w1_in = [sem(f"w1_in{n}") for n in range(GR // 2)]
        w2_in = [sem(f"w2_in{n}") for n in range(GR)]
        b_in = sem("b_in")
        v = sem("p4_v")
        pool_s = sem("p4_pool")
        based = sem("p4_based")
        merged = sem("p4_merged")
        max_s = sem("p4_max")
        exp_s = sem("p4_exp")
        idx_s_done = sem("p4_idx")
        gathered = sem("p4_gathered")
        var_s = sem("p4_var")
        rstd_s = sem("p4_rstd")
        pooled_s = sem("p4_pooled")
        pT_s = sem("p4_pT")
        pTc_s = sem("p4_pTc")
        zeroed = sem("p4_zeroed")
        turned_s = sem("p4_turned")
        hTc_s = sem("p4_hTc")
        l1_s = sem("p4_l1")
        pre_s = sem("p4_pre")
        gelu_s = sem("p4_gelu")
        l2_s = sem("p4_l2")
        diag_s = sem("p4_diag")
        ibc_s = sem("p4_ibc")
        sel_s = sem("p4_sel")
        add_s = sem("p4_add")
        scat_i = sem("p4_scat_i")
        final_s = sem("p4_final")
        scattered = sem("p4_scattered")
        block = stack.enter_context(nc.Block())
        places2 = [w1_a[:, n] for n in range(GR // 2)] + [w1_b[:, n] for n in range(GR // 2)]

        @block.sync
        def _(sp):
            sp.dma_start(b1[:], weight1[:, C, :]).then_inc(b_in, 16)
            sp.dma_start(b2[:], weight2[:, H, :]).then_inc(b_in, 16)

            sp.wait_ge(based, 1)
            for dst, src in ((mv, cand_v), (mi, cand_i)):
                for h in range(2):
                    sp.dma_start(dst[:, h], src[h * E:(h + 1) * E]).then_inc(merged, 16)
            for h in range(2):
                sp.dma_start(ms[:, h], exp_sum[h * E:(h + 1) * E]).then_inc(merged, 16)
            for g in range(GR // 2):
                sp.dma_start(w1_b[:, g], first_layer(weight1, GR // 2 + g)).then_inc(w1_in[g], 16)
            for g in range(GR):
                sp.wait_ge(l1_s, g + 1)
                for e in range(EG):
                    sp.dma_start(places2[g][:, e], weight2[g * EG + e, 0:H, :].rearrange("(c p) o -> p c o", p=P)
                                 ).then_inc(w2_in[g], 16)

        @block.gpsimd
        def _(pool):
            for h in range(2):
                pool.iota(base[h * E:(h + 1) * E], pattern=[[GT, NG], [0, K]], base=h * HALF * N,
                          channel_multiplier=0, allow_small_or_imprecise_dtypes=True)
            pool.iota(place[:], pattern=[[1, NC2]], base=0, channel_multiplier=0,
                      allow_small_or_imprecise_dtypes=True)
            pool.memset(half[:], -0.5)
            pool.memset(ones[:], 1.0).then_inc(pool_s, 1)
            pool.wait_ge(pool_s, 1)
            pool.affine_select(out=lower[:], in_=ones[:], compare_op=ALU.is_gt, fill=0.0, base=0,
                               pattern=[[-1, E]], channel_multiplier=1).then_inc(pool_s, 1)
            for k in range(K):
                pool.wait_ge(idx_s_done, k + 1)
                pool.indirect_dma_start(out=xg[:, k, :], out_offset=None, in_=out_tokens,
                                        in_offset=bass.IndirectOffsetOnAxis(ap=idx_u[:, k:k + 1], axis=0)
                                        ).then_inc(gathered, 16)
            pool.memset(spread[:], 0.0).then_inc(zeroed, 1)
            pool.wait_ge(var_s, 1)
            pool.tensor_tensor(rstd[:], var_e[:], half[:], ALU.pow).then_inc(rstd_s, 1)
            pool.wait_ge(scat_i, 1)
            pool.wait_ge(final_s, 1)
            for k in range(K):
                if k:
                    pool.wait_ge(scattered, 16 * k)
                pool.indirect_dma_start(out=out_tokens,
                                        out_offset=bass.IndirectOffsetOnAxis(ap=idx_su[:, k:k + 1], axis=0),
                                        in_=xgn[:, k, :], in_offset=None,
                                        bounds_check=TOKENS - 1, oob_is_err=False).then_inc(scattered, 16)
            pool.wait_ge(scattered, 16 * K)

        @block.vector
        def _(dve):
            count = [0]

            def link(ins):
                count[0] += 1
                ins.then_inc(v, 1)
                dve.wait_ge(v, count[0])

            dve.wait_ge(pool_s, 2)
            dve.tensor_tensor(cand_i[:], cand_i[:], base[:], ALU.add).then_inc(based, 1)
            dve.wait_ge(merged, 16 * 6)
            mvf = mv[:].rearrange("e h g k -> e (h g k)")
            mif = mi[:].rearrange("e h g k -> e (h g k)")
            link(dve.max(v8[:], mvf))
            link(dve.max_index(p8[:], v8[:], mvf))
            dve.tensor_scalar(negm[:], v8[:, 0:1], -1.0, None, ALU.mult).then_inc(max_s, 1)
            link(dve.tensor_copy(p8f[:], p8[:]))
            for k in range(K):
                link(dve.scalar_tensor_tensor(junk[:], place[:], p8f[:, k:k + 1], mif, ALU.is_equal, ALU.mult,
                                              accum_out=idx[:, k:k + 1]))
                dve.tensor_copy(idx_u[:, k:k + 1], idx[:, k:k + 1]).then_inc(idx_s_done, 1)
            dve.wait_ge(exp_s, 2)
            link(dve.tensor_tensor(eg[:], eg[:], ms[:].rearrange("e h g -> e (h g)"), ALU.mult))
            link(dve.reduce_sum(zsum[:], eg[:], axis=AX.X))
            link(dve.reciprocal(zrec[:], zsum[:]))
            link(dve.tensor_scalar(topv[:], topv[:], zrec[:], None, ALU.mult))
            for k in range(K):
                last = dve.tensor_scalar(diag[:, k, :], ident[0:E, 0:E], idx[:, k:k + 1], None, ALU.mult)
            last.then_inc(diag_s, 1)
            dve.wait_ge(ibc_s, 1)
            link(dve.tensor_copy(idx_bc[:], ps_i[:].rearrange("e (k a) -> e k a", k=K)))
            for k in range(K):
                if k == 0:
                    link(dve.tensor_scalar(sel[:, 0], idx_bc[:], idx[:, k:k + 1], topv[:, k:k + 1],
                                           ALU.is_equal, ALU.mult))
                else:
                    link(dve.tensor_scalar(sel_t[:], idx_bc[:], idx[:, k:k + 1], topv[:, k:k + 1],
                                           ALU.is_equal, ALU.mult))
                    link(dve.tensor_tensor(sel[:, k % 2], sel[:, (k - 1) % 2], sel_t[:], ALU.add))
            for k in range(K):
                link(dve.scalar_tensor_tensor(junk[:, 0:E], idx_bc[:, k, :], idx[:, k:k + 1], lower[:],
                                              ALU.is_equal, ALU.mult, accum_out=dup[:, k:k + 1]))
            link(dve.scalar_tensor_tensor(idx_s[:], dup[:], float(TOKENS), idx[:], ALU.mult, ALU.add))
            dve.tensor_copy(idx_su[:], idx_s[:]).then_inc(scat_i, 1)
            dve.wait_ge(gathered, 16 * K)
            for k in range(K):
                last = dve.bn_stats(st[:, k, :], xg[:, k, :])
            link(last)
            for k in range(K):
                last = dve.bn_aggr(mean_var[:, k, :], st[:, k, :])
            link(last)
            dve.tensor_scalar(var_e[:], mean_var[:, :, 1], LN_EPS, None, ALU.add).then_inc(var_s, 1)
            dve.wait_ge(rstd_s, 1)
            link(dve.scalar_tensor_tensor(nbias[:], mean_var[:, :, 0], -1.0, rstd[:], ALU.mult, ALU.mult))
            for k in range(K):
                last = dve.tensor_scalar(xgn[:, k, :], xg[:, k, :], rstd[:, k:k + 1], nbias[:, k:k + 1],
                                         ALU.mult, ALU.add)
            link(last)
            for k in range(K):
                if k == 0:
                    ins = dve.tensor_scalar(pooled[:], xgn[:, k, :], topv[:, k:k + 1], None, ALU.mult)
                else:
                    ins = dve.scalar_tensor_tensor(pooled[:], xgn[:, k, :], topv[:, k:k + 1], pooled[:],
                                                   ALU.mult, ALU.add)
                if k < K - 1:
                    link(ins)
            ins.then_inc(pooled_s, 1)
            dve.wait_ge(zeroed, 1)
            dve.wait_ge(pT_s, 1)
            for w in range(E // EW):
                last = dve.tensor_copy(spread[:, 0, w * EW * EW:(w + 1) * EW * EW:EW + 1], ps_p[:, w * EW:(w + 1) * EW])
            last.then_inc(pTc_s, 1)
            dve.wait_ge(l1_s, GR)
            dve.wait_ge(b_in, 32)
            dve.tensor_tensor(h_pre[:], ps_h[:], b1[:], ALU.add).then_inc(pre_s, 1)
            dve.wait_ge(turned_s, 1)
            for w in range(E // EW):
                last = dve.tensor_copy(spread[:, :, w * EW * EW:(w + 1) * EW * EW:EW + 1],
                                       ps_b[:].rearrange("p (c e) -> p c e", c=HC)[:, :, w * EW:(w + 1) * EW])
            last.then_inc(hTc_s, 1)
            dve.wait_ge(l2_s, 1)
            dve.tensor_tensor(out_e[:], ps_oe[:], b2[:], ALU.add).then_inc(sel_s, 1)
            dve.wait_ge(add_s, 1)
            for n in range(2):
                last = dve.tensor_tensor(xgn[:, 4 * n:4 * n + 4, :], ps_r[n][:].rearrange("e (k c) -> e k c", k=4),
                                         xg[:, 4 * n:4 * n + 4, :], ALU.add)
            last.then_inc(final_s, 1)

        @block.scalar
        def _(act):
            act.wait_ge(max_s, 1)
            act.activation(eg[:], mv[:].rearrange("e h g k -> e (h g) k")[:, :, 0], ACT.Exp,
                           bias=negm[:]).then_inc(exp_s, 1)
            act.activation(topv[:], v8[:], ACT.Exp, bias=negm[:]).then_inc(exp_s, 1)
            act.wait_ge(pre_s, 1)
            act.activation(h_pre[:], h_pre[:], ACT.Gelu).then_inc(gelu_s, 1)

        @block.tensor
        def _(pe):
            pe.wait_ge(diag_s, 1)
            pe.matmul(ps_i[:], ones[:], diag[:].rearrange("e k a -> e (k a)"), start=True, stop=True).then_inc(ibc_s, 1)
            pe.wait_ge(pooled_s, 1)
            pe.transpose(ps_p[:], pooled[:], ident[0:E, 0:E]).then_inc(pT_s, 1)
            pe.wait_ge(pTc_s, 1)
            for g in range(GR):
                if g >= GR // 2:
                    pe.wait_ge(w1_in[g - GR // 2], 16)
                w1 = w1_a[:, g] if g < GR // 2 else w1_b[:, g - GR // 2]
                for x in range(EG):
                    e = g * EG + x
                    rows = slice(e // EW * EW, (e // EW + 1) * EW)
                    last = pe.matmul(ps_h[rows, :], spread[:, 0, e * EW:(e + 1) * EW], w1[:, x, :],
                                     start=(e % EW == 0), stop=(e % EW == EW - 1))
                last.then_inc(l1_s, 1)
            pe.wait_ge(gelu_s, 1)
            for c in range(HC):
                last = pe.transpose(ps_b[:, c * E:(c + 1) * E], h_pre[:, c * P:(c + 1) * P], ident[0:E, 0:E])
            last.then_inc(turned_s, 1)
            pe.wait_ge(hTc_s, 1)
            for e in range(E):
                if e % EG == 0:
                    pe.wait_ge(w2_in[e // EG], 16 * EG)
                w2 = places2[e // EG][:, e % EG].rearrange("p (c o) -> p c o", c=HC)
                rows = slice(e // EW * EW, (e // EW + 1) * EW)
                for c in range(HC):
                    last = pe.matmul(ps_oe[rows, :], spread[:, c, e * EW:(e + 1) * EW], w2[:, c, :],
                                     start=(e % EW == 0 and c == 0), stop=(e % EW == EW - 1 and c == HC - 1))
            last.then_inc(l2_s, 1)
            pe.wait_ge(sel_s, 1)
            for k in range(K):
                last = pe.matmul(ps_r[k // 4][:, k % 4 * C:(k % 4 + 1) * C], sel[:, (K - 1) % 2, k, :], out_e[:],
                                 start=True, stop=True)
            last.then_inc(add_s, 1)


_INS = ['x', 'L0_conv_mask', 'L0_conv_ln_g', 'L0_conv_ln_b', 'L0_conv_Wl', 'L0_conv_bl', 'L0_conv_Wr',
        'L0_conv_br', 'L0_conv_Wgl', 'L0_conv_bgl', 'L0_conv_Wgr', 'L0_conv_bgr', 'L0_conv_cg', 'L0_conv_cb',
        'L0_conv_Wo', 'L0_conv_bo', 'L0_conv_Wg', 'L0_conv_bg', 'L0_ffn_gate_w', 'L0_ffn_gate_b',
        'L0_ffn_weight1', 'L0_ffn_weight2']
_OUTS = [((1, N, N, C), 'float32')]


def kernel(**inputs):
    import numpy as _np
    import concourse.bacc as _bacc
    from concourse import mybir as _mybir
    from concourse.bass_utils import run_bass_kernel_spmd as _run

    nc = _bacc.Bacc("TRN2", target_bir_lowering=False, num_devices=1)
    arrays, args = {}, []
    for name in _INS:
        a = _np.ascontiguousarray(inputs[name])
        arrays[f"in_{name}_dram"] = a
        args.append(nc.dram_tensor(f"in_{name}_dram", a.shape, _mybir.dt.from_np(a.dtype), kind="ExternalInput").ap())
    for i, (shape, dtype) in enumerate(_OUTS):
        args.append(nc.dram_tensor(f"out_{i}_dram", shape, _mybir.dt.from_np(_np.dtype(dtype)),
                                   kind="ExternalOutput").ap())
    mk_metaformer(nc, *args)
    r = _run(nc, [arrays], core_ids=[0])
    return r.results[0]["out_0_dram"]
```
